# Optimizing a Trainium2 kernel written in Bass

```python
import numpy as np
import jax
import jax.numpy as jnp

def _softmax(x, axis=-1):
    return jax.nn.softmax(x, axis=axis)

def _gelu(x):
    return jax.nn.gelu(x, approximate=True)

def _silu(x):
    return jax.nn.silu(x)

def _sigmoid(x):
    return jax.nn.sigmoid(x)

def _layernorm(x, axis=-1, eps=1e-05):
    m = jnp.mean(x, axis=axis, keepdims=True)
    v = jnp.var(x, axis=axis, keepdims=True)
    return (x - m) / jnp.sqrt(v + eps)

def _scatter_add(tgt, idx, src, axis=0):
    return tgt.at[idx].add(src)

def _segment_sum(src, seg, n):
    return jax.ops.segment_sum(src, seg, n)
kernel_name = 'mk_xattn_ffn_d1_seqx_r4_57d4df'

def setup_inputs(seed: int=0):
    np.random.seed(seed)
    _w = jnp.asarray

    def _rec_inputs():
        import jax
        import jax.numpy as jnp
        _rk = jax.random.key(seed)
        x = 7.22e-05 + 1 * jax.random.normal(jax.random.fold_in(_rk, 1), (16, 112, 256), jnp.float32)
        _lenS = 112 - jax.random.randint(jax.random.fold_in(_rk, 7), (16,), 0, max(1, 112 // 4) + 1, jnp.int32)
        _lenS2 = 375 - jax.random.randint(jax.random.fold_in(_rk, 8), (16,), 0, max(1, 375 // 4) + 1, jnp.int32)
        _ctx_1024P = jax.random.normal(jax.random.fold_in(_rk, 11), (16, 16, 256), jnp.float32)
        _ctx_1024c = jax.random.dirichlet(jax.random.fold_in(_rk, 511), 0.3 * jnp.ones((16,), jnp.float32), (16, 375))
        _ctx_1024t = jnp.einsum('bsk,bkd->bsd', _ctx_1024c, _ctx_1024P)
        _ctx_1024t = _ctx_1024t * jax.lax.rsqrt(jnp.mean(jnp.square(_ctx_1024t)) + 1e-12) * 0.953939
        ctx_1024 = 4.13588e-05 + 0.999923 * (_ctx_1024t + 0.3 * jax.random.normal(jax.random.fold_in(_rk, 611), (16, 375, 256), jnp.float32))
        _validS = jnp.arange(112)[None, :] < _lenS[:, None]
        _validS2 = jnp.arange(375)[None, :] < _lenS2[:, None]
        _causal = jnp.tril(jnp.ones((112, 112), dtype=bool))
        mask_BxS2_ik0 = jnp.where(jnp.broadcast_to(_validS2[:, :], (16, 375)), 0, 1).astype(jnp.int32)
        return (x, ctx_1024, mask_BxS2_ik0)
    x, ctx_1024, mask_BxS2_ik0 = _rec_inputs()

    def _L0_xattn_setup():
        import jax, jax.numpy as jnp
        import numpy as np
        import math
        H = 16
        D_MODEL = 256
        D_K = D_MODEL // H
        B, S = (4, 512)
        NEG = -1000000000.0

        def _split_heads(x):
            b, s, _ = x.shape
            return x.reshape(b, s, H, D_K).transpose(0, 2, 1, 3)
        key = jax.random.key(seed)
        ks = jax.random.split(key, 13)
        scale = 1.0 / math.sqrt(D_MODEL)
        inp = {'query': jax.random.normal(ks[0], (B, S, D_MODEL), jnp.float32), 'key': jax.random.normal(ks[1], (B, S, D_MODEL), jnp.float32), 'value': jax.random.normal(ks[2], (B, S, D_MODEL), jnp.float32), 'mask': jax.random.randint(ks[3], (B, S), 0, 2, jnp.int32), 'Wq': jax.random.normal(ks[4], (D_MODEL, D_MODEL), jnp.float32) * scale, 'bq': jax.random.normal(ks[5], (D_MODEL,), jnp.float32) * scale, 'Wk': jax.random.normal(ks[6], (D_MODEL, D_MODEL), jnp.float32) * scale, 'bk': jax.random.normal(ks[7], (D_MODEL,), jnp.float32) * scale, 'Wv': jax.random.normal(ks[8], (D_MODEL, D_MODEL), jnp.float32) * scale, 'bv': jax.random.normal(ks[9], (D_MODEL,), jnp.float32) * scale, 'Wo': jax.random.normal(ks[10], (D_MODEL, D_MODEL), jnp.float32) * scale, 'bo': jax.random.normal(ks[11], (D_MODEL,), jnp.float32) * scale}
        return inp
    _L0_xattn_all = _L0_xattn_setup()
    _L0_xattn_in = {k: v for k, v in _L0_xattn_all.items() if k in ('Wq', 'bq', 'Wk', 'bk', 'Wv', 'bv', 'Wo', 'bo')}
    del _L0_xattn_all

    def _L0_ffn_setup():
        import jax, jax.numpy as jnp
        import numpy as np
        EPS = 1e-09
        key = jax.random.key(seed)
        k0, k1, k2, k3 = jax.random.split(key, 4)
        B, S, H, F, E = (4, 512, 256, 512, 8)
        return {'hidden_states': jax.random.normal(k0, (B, S, H), dtype=jnp.float32), 'router_w': jax.random.normal(k1, (H, E), dtype=jnp.float32) * 0.02, 'w1': jax.random.normal(k2, (E, H, F), dtype=jnp.float32) * 0.02, 'w2': jax.random.normal(k3, (E, F, H), dtype=jnp.float32) * 0.02}
    _L0_ffn_all = _L0_ffn_setup()
    _L0_ffn_in = {k: v for k, v in _L0_ffn_all.items() if k in ('router_w', 'w1', 'w2')}
    del _L0_ffn_all
    return {'x': x, 'ctx_1024': ctx_1024, 'mask_BxS2_ik0': mask_BxS2_ik0, 'L0_xattn_Wq': _L0_xattn_in['Wq'], 'L0_xattn_bq': _L0_xattn_in['bq'], 'L0_xattn_Wk': _L0_xattn_in['Wk'], 'L0_xattn_bk': _L0_xattn_in['bk'], 'L0_xattn_Wv': _L0_xattn_in['Wv'], 'L0_xattn_bv': _L0_xattn_in['bv'], 'L0_xattn_Wo': _L0_xattn_in['Wo'], 'L0_xattn_bo': _L0_xattn_in['bo'], 'L0_ffn_router_w': _L0_ffn_in['router_w'], 'L0_ffn_w1': _L0_ffn_in['w1'], 'L0_ffn_w2': _L0_ffn_in['w2']}

def reference(x, ctx_1024, mask_BxS2_ik0, L0_xattn_Wq, L0_xattn_bq, L0_xattn_Wk, L0_xattn_bk, L0_xattn_Wv, L0_xattn_bv, L0_xattn_Wo, L0_xattn_bo, L0_ffn_router_w, L0_ffn_w1, L0_ffn_w2):
    import jax
    import jax.numpy as jnp

    def _L0_xattn_ref(query, key, value, mask, Wq, bq, Wk, bk, Wv, bv, Wo, bo):
        import jax, jax.numpy as jnp
        import numpy as np
        import math
        H = 16
        D_MODEL = 256
        D_K = D_MODEL // H
        B, S = (4, 512)
        NEG = -1000000000.0

        def _split_heads(x):
            b, s, _ = x.shape
            return x.reshape(b, s, H, D_K).transpose(0, 2, 1, 3)
        q = _split_heads(query @ Wq.T + bq)
        k = _split_heads(key @ Wk.T + bk)
        v = _split_heads(value @ Wv.T + bv)
        scores = jnp.einsum('bhqd,bhkd->bhqk', q, k) / math.sqrt(D_K)
        m = mask[:, None, None, :]
        scores = jnp.where(m == 0, NEG, scores)
        p = jax.nn.softmax(scores, axis=-1)
        out = jnp.einsum('bhqk,bhkd->bhqd', p, v)
        out = out.transpose(0, 2, 1, 3).reshape(query.shape[0], -1, D_MODEL)
        return out @ Wo.T + bo

    def _L0_ffn_ref(hidden_states, router_w, w1, w2):
        import jax, jax.numpy as jnp
        import numpy as np
        EPS = 1e-09
        TOP_K = 2
        orig_shape = hidden_states.shape
        H = orig_shape[-1]
        E = router_w.shape[-1]
        flat = hidden_states.reshape(-1, H)
        T = flat.shape[0]
        gate_logits = flat @ router_w
        gate_probs = jax.nn.softmax(gate_logits, axis=-1)
        topk_w, topk_idx = jax.lax.top_k(gate_probs, TOP_K)
        topk_w = topk_w / jnp.clip(topk_w.sum(-1, keepdims=True), EPS)
        cw = jnp.zeros((T, E), dtype=flat.dtype).at[jnp.arange(T)[:, None], topk_idx].add(topk_w)
        h = jax.nn.silu(jnp.einsum('td,edf->etf', flat, w1))
        y = jnp.einsum('etf,efd->etd', h, w2)
        out = jnp.einsum('etd,te->td', y, cw)
        return out.reshape(orig_shape)
    x = x + _L0_xattn_ref(_layernorm(x, axis=-1), ctx_1024, ctx_1024, mask_BxS2_ik0, L0_xattn_Wq, L0_xattn_bq, L0_xattn_Wk, L0_xattn_bk, L0_xattn_Wv, L0_xattn_bv, L0_xattn_Wo, L0_xattn_bo)
    x = x + _L0_ffn_ref(_layernorm(x, axis=-1), L0_ffn_router_w, L0_ffn_w1, L0_ffn_w2)
    return x

_drawn_inputs = setup_inputs


def setup_inputs(seed=0):
    import zlib

    import numpy as np

    out = dict(_drawn_inputs(seed))
    spreads = {}
    factors = {'L0_xattn_bq': 3.8, 'L0_xattn_bk': 8.0}
    for name, (base, spread) in spreads.items():
        noise = np.random.default_rng([zlib.crc32(name.encode()), seed]).standard_normal(out[name].shape)
        drawn = base * np.exp(spread * noise) if base else spread * noise
        out[name] = jnp.asarray(drawn.astype(out[name].dtype))
    for name, factor in factors.items():
        out[name] = (out[name] * factor).astype(out[name].dtype)
    return out
```

```python
from contextlib import ExitStack

import concourse.bass as bass
from concourse import mybir

F32 = mybir.dt.float32
F32R = mybir.dt.float32r
I32 = mybir.dt.int32
ALU = mybir.AluOpType
ACT = mybir.ActivationFunctionType
AX = mybir.AxisListType

P = 128
B, S, D = 16, 112, 256
C = 375
CP = C + 1
H, DK = 16, 16
E, F = 8, 512
KD = D // P
KF = F // P
KT = 3
CT = C // KT
PAIRS = H // 2
QUADS = H // 4
T = B * S
NT = T // P
GB = 4
NG = B // GB
SG = GB * S
TG = 2 * P
NTG = T // TG
STEPS = E * NTG
NEG = -1.0e9
NEG_HI = -1000079360.0
NEG_LO = NEG - NEG_HI
LN_EPS = 1e-5
GATE_EPS = 1e-9

R_MASK, R_MAX, ROWS = 96, 98, 100

BK_ST, BK_MAX, BK_KV, BK_OUT = 0, 3, 5, 7


class Batch:

    def __init__(self, i, off):
        self.i, self.off = i, off
        self.par, self.turn, self.n = off % 2, i + off // 2, 2 * i + off

    def after(self, k):
        return Batch(self.i, self.off + k)


def xattn_moe_kernel(nc, x_rows, x_tiles, ctx_t, mask, wq_t, wk_t, wv_t, wo_t, bq, bk, bv, bo,
                     router_w, w1, w2, out):
    ctx = ExitStack()
    with ctx:
        def sem(name):
            return ctx.enter_context(nc.semaphore(name))

        base = (nc.sbuf_base + 63) // 64 * 64
        cursor = {"at": base, "top": base}

        def sb(name, shape, dt=F32):
            size = 4
            for n in shape[1:]:
                size *= n
            off = cursor["at"]
            cursor["at"] += (size + 63) // 64 * 64
            cursor["top"] = max(cursor["top"], cursor["at"])
            return nc.alloc_sbuf_tensor_at(name, shape, dt, offset=off)

        ident = sb("ident", [P, P])
        x2 = sb("x2", [P, NT, D])
        th = sb("attn_t_hi", [P, KD, T], F32R)
        tl = sb("attn_t_lo", [P, KD, T], F32R)
        wh = sb("attn_w_hi", [P, 4, KD, D], F32R)
        wl = sb("attn_w_lo", [P, 4, KD, D], F32R)
        rw_raw = sb("router_raw", [P, KD, E])
        rwh = sb("router_hi", [P, KD, E], F32R)
        rwl = sb("router_lo", [P, KD, E], F32R)
        bv_b = sb("bv_b", [P, D])
        bo_b = sb("bo_b", [P, D])
        bq_c = sb("bq_c", [P, KD])
        bk_c = sb("bk_c", [P, KD])
        mask_c = sb("mask_c", [2, 2])
        stats = sb("stats", [P, B, 6])
        moments = sb("moments", [P, B, 2])
        std = sb("std", [P, B])
        rstd = sb("rstd", [P, B])
        eps_c = sb("eps_c", [P, 1])
        w1_raw = sb("w1_raw", [P, KD, F])
        w2_raw = sb("w2_raw", [P, KF, D])
        wraw = [w1_raw[:, 0:2, 0:256], w1_raw[:, 0:2, 256:512], w2_raw[:, 0:2, :], w2_raw[:, 2:4, :]]

        shared = cursor["at"]
        xr = sb("x_rows_sb", [S, B, D])
        xh = [sb(f"x_t_hi{p}", [P, KD, SG], F32R) for p in range(2)]
        xl = [sb(f"x_t_lo{p}", [P, KD, SG], F32R) for p in range(2)]
        qf = sb("q_f32", [P, KD, SG])
        q_end = cursor["at"]
        cursor["at"] = shared
        w1h = [sb(f"w1_hi{p}", [P, KD, F], F32R) for p in range(2)]
        w1l = [sb(f"w1_lo{p}", [P, KD, F], F32R) for p in range(2)]
        w2h = [sb(f"w2_hi{p}", [P, KF, D], F32R) for p in range(2)]
        w2l = [sb(f"w2_lo{p}", [P, KF, D], F32R) for p in range(2)]
        cursor["at"] = max(q_end, cursor["at"])

        attn_start = cursor["at"]
        c_raw = [sb(f"ctx_raw{p}", [P, KD, CP]) for p in range(2)]
        ch = [sb(f"ctx_hi{p}", [P, KD, CP], F32R) for p in range(2)]
        cl = [sb(f"ctx_lo{p}", [P, KD, CP], F32R) for p in range(2)]
        m_raw = [sb(f"mask_raw{p}", [P, CP], I32) for p in range(2)]
        keep = [sb(f"keep{p}", [P, CP]) for p in range(2)]
        m_row = [sb(f"mask_row{p}", [2, CP], F32R) for p in range(2)]
        kf = sb("k_f32", [P, KD, CP])
        kh = sb("k_hi", [P, KD, CP], F32R)
        kl = sb("k_lo", [P, KD, CP], F32R)
        ks = [sb(f"k_stack{p}", [P, PAIRS, CP], F32R) for p in range(2)]
        qs = [sb(f"q_stack{p}", [P, PAIRS, 2 * S], F32R) for p in range(2)]
        v1 = [sb(f"v_ones{p}", [CT, KT, H, DK + 1]) for p in range(2)]
        q_hl_at = cursor["at"]
        pr = [sb(f"probs{p}", [CT, KT, 4 * S]) for p in range(2)]
        cursor["at"] = max(cursor["at"], q_hl_at)
        neg_max = sb("neg_max", [S, H])
        mx_h = sb("max_hi", [H, S], F32R)
        mx_l = sb("max_lo", [H, S], F32R)
        rsum = sb("rsum", [S, H])
        an = sb("attn_rows", [S, D])
        attn_end = cursor["at"]
        cursor["at"] = q_hl_at
        qh = [sb(f"q_hi{p}", [P, KD, SG], F32R) for p in range(1)]
        ql = [sb(f"q_lo{p}", [P, KD, SG], F32R) for p in range(1)]
        assert cursor["at"] <= q_hl_at + 2 * KT * 4 * S * 4
        cursor["at"] = attn_start
        hf = [sb(f"h_f32{p}", [P, KF, TG]) for p in range(2)]
        hh = [sb(f"h_hi{p}", [P, KF, TG], F32R) for p in range(2)]
        hl = [sb(f"h_lo{p}", [P, KF, TG], F32R) for p in range(2)]
        fh = sb("flat_t_hi", [P, KD, T], F32R)
        fl = sb("flat_t_lo", [P, KD, T], F32R)
        xn2 = sb("xn2", [P, NT, D])
        gates = [sb(f"gate{n}", [P, NT, E]) for n in range(8)]
        gcol = [sb(f"gate_col{n}", [P, NT]) for n in range(4)]
        cw = sb("gate_weights", [P, NT, E])
        assert cursor["top"] <= nc.sbuf_usable_end, (cursor, nc.sbuf_usable_end)

        ps = ctx.enter_context(nc.psum_tensor("ps", [P, 8, 512], F32))

        k_scratch = [nc.dram_tensor(f"k_scratch{p}", [2, KD, P, CP], F32).ap() for p in range(2)]
        q_scratch = nc.dram_tensor("q_scratch", [2, KD, P, T], F32).ap()

        aw_in = [sem(f"aw_in{n}") for n in range(4)]
        bias_in, xr_in, x2_in, rw_in = sem("bias_in"), sem("xr_in"), sem("x2_in"), sem("rw_in")
        ctx_in = [sem(f"ctx_in{p}") for p in range(2)]
        ew_in = sem("ew_in")
        zeros_set, const_set, ident_set, filled = sem("zeros_set"), sem("const_set"), sem("ident_set"), sem("filled")
        wh_ready, wl_ready = sem("wh_ready"), sem("wl_ready")
        ch_ready, cl_ready = sem("ch_ready"), sem("cl_ready")
        keep_ready, mrow_ready = sem("keep_ready"), sem("mrow_ready")
        kproj_done, kf_ready, kh_ready, kl_ready = sem("kproj_done"), sem("kf_ready"), sem("kh_ready"), sem("kl_ready")
        k_written = [sem(f"k_written{p}") for p in range(2)]
        k_stacked = [sem(f"k_stacked{p}") for p in range(2)]
        q_stacked = [sem(f"q_stacked{p}") for p in range(2)]
        vproj_done, v_ready = sem("vproj_done"), sem("v_ready")
        smax_done, max_read, maxt_done, mx_ready = sem("smax_done"), sem("max_read"), sem("maxt_done"), sem("mx_ready")
        mx_stacked = [sem(f"mx_stacked{p}") for p in range(2)]
        st_done, p_ready, pv_done = sem("st_done"), sem("p_ready"), sem("pv_done")
        rsum_ready, an_ready, at_done = sem("rsum_ready"), sem("an_ready"), sem("at_done")
        th_ready, tl_ready = sem("th_ready"), sem("tl_ready")
        stats_ready, mom_ready, std_ready, rstd_ready, xn_ready = (
            sem("stats_ready"), sem("mom_ready"), sem("std_ready"), sem("rstd_ready"), sem("xn_ready"))
        xt_done, xh_ready, xl_ready = sem("xt_done"), sem("xh_ready"), sem("xl_ready")
        qproj_done, qf_ready, qh_ready, ql_ready = sem("qproj_done"), sem("qf_ready"), sem("qh_ready"), sem("ql_ready")
        q_written = sem("q_written")
        xb_ready, oproj_done = sem("xb_ready"), sem("oproj_done")
        st2_ready, mom2_ready, std2_ready, rstd2_ready, xn2_ready = (
            sem("st2_ready"), sem("mom2_ready"), sem("std2_ready"), sem("rstd2_ready"), sem("xn2_ready"))
        ft_done, fh_ready, fl_ready, route_done = sem("ft_done"), sem("fh_ready"), sem("fl_ready"), sem("route_done")
        rw_ready = sem("rw_ready")
        gate_step, gate_exp, cw_ready = sem("gate_step"), sem("gate_exp"), sem("cw_ready")
        ew_ready = sem("ew_ready")
        h_done, hf_ready, hh_ready, hl_ready, y_done, x2_added = (
            sem("h_done"), sem("hf_ready"), sem("hh_ready"), sem("hl_ready"), sem("y_done"), sem("x2_added"))
        out_written = sem("out_written")

        block = ctx.enter_context(nc.Block())

        @block.sync
        def _(sp):
            def load_ctx(b):
                if not (isinstance(b.n, int) and b.n < 2):
                    sp.wait_ge(ch_ready, b.n - 1)
                    sp.wait_ge(cl_ready, b.n - 1)
                    sp.wait_ge(keep_ready, b.n - 1)
                for k in range(KD):
                    sp.dma_start(c_raw[b.par][:, k, 0:C], ctx_t[k, :, bass.ds(b.n, 1), :]
                                 .rearrange("p a n -> p (a n)")).then_inc(ctx_in[b.par], 16)
                sp.dma_start(m_raw[b.par][:, 0:C], mask[bass.ds(b.n, 1), :].to_broadcast([P, C]))\
                    .then_inc(ctx_in[b.par], 16)

            def stack_queries(b):
                if not (isinstance(b.n, int) and b.n < 2):
                    sp.wait_ge(st_done, QUADS * (b.n - 1))
                for c, part in ((0, 0), (1, 0), (2, 1)):
                    for a in range(2):
                        sp.dma_start(
                            qs[b.par][32 * c + 16 * a:32 * c + 16 * a + 16, :, S * a:S * a + S].bitcast(F32),
                            q_scratch[part, :, :, bass.ds(S * b.n, S)]
                            .rearrange("t (q s) n -> s (t q) n", q=4)[16 * a:16 * a + 16])\
                            .then_inc(q_stacked[b.par], 16)

            def stack_keys(b):
                sp.wait_ge(kh_ready, b.n + 1)
                sp.wait_ge(kl_ready, b.n + 1)
                if not (isinstance(b.n, int) and b.n < 2):
                    sp.wait_ge(k_stacked[b.par], 64 * b.turn)
                    sp.wait_ge(st_done, QUADS * (b.n - 1))
                for part, src in ((0, kh), (1, kl)):
                    sp.dma_start(k_scratch[b.par][part].rearrange("t p n -> p t n"), src[:, :, :].bitcast(F32))\
                        .then_inc(k_written[b.par], 16)
                sp.wait_ge(mrow_ready, b.n + 1)
                sp.dma_start(ks[b.par][R_MASK:R_MASK + 2, :, :].bitcast(F32),
                             m_row[b.par][:, :].bitcast(F32).rearrange("p (a n) -> p a n", a=1)
                             .to_broadcast([2, PAIRS, CP])).then_inc(k_stacked[b.par], 16)
                sp.wait_ge(k_written[b.par], 32 * (b.turn + 1))
                for c, part in ((0, 0), (1, 1), (2, 0)):
                    sp.dma_start(ks[b.par][32 * c:32 * c + 32, :, :].bitcast(F32),
                                 k_scratch[b.par][part].rearrange("t (q s) n -> s (t q) n", q=4))\
                        .then_inc(k_stacked[b.par], 16)

            def stack_max(b):
                sp.wait_ge(mx_ready, 2 * (b.n + 1))
                for r, src in ((0, mx_h), (1, mx_l)):
                    sp.dma_start(qs[b.par][R_MAX + r:R_MAX + r + 1, :, :].bitcast(F32)
                                 .rearrange("p q (a n) -> p (q a) n", a=2),
                                 src[:, :].bitcast(F32)).then_inc(mx_stacked[b.par], 16)

            def turn(b, last=False, ahead=3):
                stack_max(b)
                if last:
                    return
                stack_queries(b.after(1))
                if ahead == 3:
                    load_ctx(b.after(3))
                stack_keys(b.after(1))

            sp.dma_start(wraw[0], wk_t.rearrange("k p n -> p k n")).then_inc(aw_in[0], 16)
            first = Batch(0, 0)
            sp.wait_ge(zeros_set, 1)
            load_ctx(first)
            sp.dma_start(bk_c[:, :], bk).then_inc(bias_in, 16)
            sp.dma_start(wraw[1], wv_t.rearrange("k p n -> p k n")).then_inc(aw_in[1], 16)
            sp.dma_start(xr[:, :, :], x_rows.rearrange("b s d -> s b d")).then_inc(xr_in, 16)
            load_ctx(first.after(1))
            sp.dma_start(bv_b[:, :], bv.to_broadcast([P, D])).then_inc(bias_in, 16)
            sp.dma_start(bo_b[:, :], bo.to_broadcast([P, D])).then_inc(bias_in, 16)
            sp.dma_start(bq_c[:, :], bq).then_inc(bias_in, 16)
            sp.dma_start(wraw[2], wq_t.rearrange("k p n -> p k n")).then_inc(aw_in[2], 16)
            sp.dma_start(wraw[3], wo_t.rearrange("k p n -> p k n")).then_inc(aw_in[3], 16)
            sp.dma_start(rw_raw[:, :, :], router_w.rearrange("k p n -> p k n")).then_inc(rw_in, 16)
            sp.dma_start(x2[:, :, :], x_tiles.rearrange("n p d -> p n d")).then_inc(x2_in, 16)
            sp.wait_ge(filled, 8)
            stack_keys(first)
            load_ctx(first.after(2))
            for g in range(NG):
                sp.wait_ge(qh_ready, g + 1)
                sp.wait_ge(ql_ready, g + 1)
                for part, src in ((0, qh[0]), (1, ql[0])):
                    sp.dma_start(q_scratch[part, :, :, SG * g:SG * g + SG].rearrange("t p n -> p t n"),
                                 src[:, :, :].bitcast(F32)).then_inc(q_written, 16)
            sp.wait_ge(q_written, 32 * NG)
            stack_queries(first)
            turn(first)
            with sp.Fori(0, (B - 4) // 2) as i:
                for off in (1, 2):
                    turn(Batch(i, off))
            turn(Batch(0, B - 3), ahead=2)
            turn(Batch(0, B - 2), ahead=2)
            turn(Batch(0, B - 1), last=True)

            def load_experts(e, first_one=False):
                sp.wait_ge(ew_ready, 4 * e)
                sp.dma_start(w1_raw[:, :, :], w1[bass.ds(e, 1), :, :, :].rearrange("a k p n -> p (a k) n"))\
                    .then_inc(ew_in, 16)
                sp.dma_start(w2_raw[:, :, :], w2[bass.ds(e, 1), :, :, :].rearrange("a k p n -> p (a k) n"))\
                    .then_inc(ew_in, 16)

            sp.wait_ge(wh_ready, 4)
            sp.wait_ge(wl_ready, 4)
            sp.dma_start(w1_raw[:, :, :], w1[0].rearrange("k p n -> p k n")).then_inc(ew_in, 16)
            sp.dma_start(w2_raw[:, :, :], w2[0].rearrange("k p n -> p k n")).then_inc(ew_in, 16)
            with sp.Fori(1, E) as e:
                load_experts(e)
            for g in range(NTG):
                sp.wait_ge(x2_added, NT + 2 * ((E - 1) * NTG + g + 1))
                sp.dma_start(out[2 * g:2 * g + 2].rearrange("n p d -> p n d"), x2[:, 2 * g:2 * g + 2, :])\
                    .then_inc(out_written, 16)
            sp.wait_ge(out_written, 16 * NTG)

        @block.gpsimd
        def _(pool):
            for p in range(2):
                pool.memset(c_raw[p][:, :, C:CP], 0.0)
                last = pool.memset(m_raw[p][:, C:CP], 0)
            last.then_inc(zeros_set, 1)
            pool.memset(eps_c[:, :], LN_EPS)
            pool.memset(ident[:, :], 0.0).then_inc(ident_set, 1)
            pool.wait_ge(ident_set, 1)
            pool.affine_select(out=ident[:, :], in_=ident[:, :], compare_op=ALU.not_equal, fill=1.0, base=0,
                               pattern=[[-1, P]], channel_multiplier=1).then_inc(ident_set, 1)

            def ctx_low(b):
                pool.wait_ge(ch_ready, b.n + 1)
                if not (isinstance(b.n, int) and b.n < 2):
                    pool.wait_ge(vproj_done, 2 * (b.n - 1))
                pool.tensor_tensor(cl[b.par][:, :, :], c_raw[b.par][:, :, :], ch[b.par][:, :, :].bitcast(F32),
                                   ALU.subtract).then_inc(cl_ready, 1)

            def key_low(b):
                pool.wait_ge(kh_ready, b.n + 1)
                if not (isinstance(b.n, int) and b.n < 1):
                    before = b.after(-1)
                    pool.wait_ge(k_written[before.par], 32 * (before.turn + 1))
                pool.tensor_tensor(kl[:, :, :], kf[:, :, :], kh[:, :, :].bitcast(F32), ALU.subtract)\
                    .then_inc(kl_ready, 1)

            first = Batch(0, 0)
            ctx_low(first)
            pool.wait_ge(cl_ready, 1)
            fills = [(ks[p][R_MASK:ROWS, :, :].bitcast(F32), 1.0) for p in range(2)]
            fills += [(v1[p][:, :, :, DK:DK + 1], 1.0) for p in range(2)]
            fills += [(qs[p][0:R_MASK, :, :].bitcast(F32), 0.0) for p in range(2)]
            fills += [(qs[p][R_MASK:ROWS, :, :].bitcast(F32), 1.0) for p in range(2)]
            for n, (what, value) in enumerate(fills):
                pool.memset(what, value).then_inc(filled, 1)
                pool.wait_ge(filled, n + 1)
            ctx_low(first.after(1))
            key_low(first)

            def turn(b, two=True):
                key_low(b.after(1))
                if two:
                    ctx_low(b.after(2))

            turn(first)
            pool.wait_ge(x2_in, 16)
            pool.wait_ge(bias_in, 64)
            for n in range(NT):
                last = pool.tensor_tensor(x2[:, n, :], x2[:, n, :], bo_b[:, :], ALU.add)
            last.then_inc(xb_ready, 1)
            with pool.Fori(0, (B - 4) // 2) as i:
                for off in (1, 2):
                    turn(Batch(i, off))
            turn(Batch(0, B - 3))
            turn(Batch(0, B - 2), two=False)

            def split_expert(e, par):
                pool.wait_ge(ew_in, 32 * (e + 1))
                if not isinstance(e, int) or e >= 2:
                    pool.wait_ge(y_done, NTG * (e - 1))
                pool.tensor_copy(w1h[par][:, :, :], w1_raw[:, :, :]).then_inc(ew_ready, 1)
                pool.tensor_copy(w2h[par][:, :, :], w2_raw[:, :, :]).then_inc(ew_ready, 1)
                pool.wait_ge(ew_ready, 4 * e + 2)
                pool.tensor_tensor(w1l[par][:, :, :], w1_raw[:, :, :], w1h[par][:, :, :].bitcast(F32),
                                   ALU.subtract).then_inc(ew_ready, 1)
                pool.tensor_tensor(w2l[par][:, :, :], w2_raw[:, :, :], w2h[par][:, :, :].bitcast(F32),
                                   ALU.subtract).then_inc(ew_ready, 1)

            pool.wait_ge(ql_ready, NG)
            pool.wait_ge(qproj_done, 2 * NG)
            for e in range(E):
                split_expert(e, e % 2)

        @block.scalar
        def _(act):
            def attn_weight(n):
                act.wait_ge(aw_in[n], 16)
                act.copy(wh[:, n, :, :], wraw[n]).then_inc(wh_ready, 1)

            def ctx_high(b):
                act.wait_ge(ctx_in[b.par], 48 * (b.turn + 1))
                if not (isinstance(b.n, int) and b.n < 2):
                    act.wait_ge(vproj_done, 2 * (b.n - 1))
                else:
                    act.wait_ge(zeros_set, 1)
                act.copy(ch[b.par][:, :, :], c_raw[b.par][:, :, :]).then_inc(ch_ready, 1)

            def key_high(b):
                act.wait_ge(kf_ready, 2 * (b.n + 1))
                if not (isinstance(b.n, int) and b.n < 1):
                    before = b.after(-1)
                    act.wait_ge(k_written[before.par], 32 * (before.turn + 1))
                act.copy(kh[:, :, :], kf[:, :, :]).then_inc(kh_ready, 1)

            def attn_high(b):
                act.wait_ge(at_done, b.n + 1)
                act.copy(th[:, :, bass.ds(S * b.n, S)],
                         ps[:, BK_OUT, 0:KD * S].rearrange("p (k n) -> p k n", k=KD)).then_inc(th_ready, 1)

            def exps(b, j):
                act.wait_ge(st_done, QUADS * b.n + j + 1)
                if not (isinstance(b.n, int) and b.n < 1 and j < 2):
                    act.wait_ge(pv_done, QUADS * b.n + j - 1)
                act.activation(pr[j % 2][:, :, :], ps[0:CT, BK_ST:BK_ST + KT, 0:4 * S], ACT.Exp)\
                    .then_inc(p_ready, 1)

            attn_weight(0)
            first = Batch(0, 0)
            ctx_high(first)
            attn_weight(1)
            ctx_high(first.after(1))
            attn_weight(2)
            attn_weight(3)
            act.wait_ge(rw_in, 16)
            act.copy(rwh[:, :, :], rw_raw[:, :, :]).then_inc(rw_ready, 1)
            act.wait_ge(mom_ready, B)
            act.wait_ge(ident_set, 1)
            act.activation(std[0:S, :], moments[0:S, :, 1], ACT.Sqrt, bias=eps_c[0:S, :]).then_inc(std_ready, 1)
            key_high(first)

            def x_high(g):
                act.wait_ge(xt_done, g + 1)
                if g >= 2:
                    act.wait_ge(qproj_done, 2 * (g - 1))
                act.copy(xh[g % 2][:, :, :], ps[:, 0:2, 0:SG]).then_inc(xh_ready, 1)

            def q_high(g):
                act.wait_ge(qf_ready, 2 * (g + 1))
                if g >= 1:
                    act.wait_ge(q_written, 32 * g)
                act.copy(qh[0][:, :, :], qf[:, :, :]).then_inc(qh_ready, 1)

            x_high(0)
            for g in range(NG):
                if g + 1 < NG:
                    x_high(g + 1)
                q_high(g)
            act.wait_ge(q_written, 32 * NG)

            def turn(b, one=True, two=True, prev=True):
                if one:
                    key_high(b.after(1))
                if prev:
                    attn_high(b.after(-1))
                exps(b, 0)
                exps(b, 1)
                if two:
                    ctx_high(b.after(2))
                exps(b, 2)
                exps(b, 3)

            turn(first, prev=False)
            with act.Fori(0, (B - 4) // 2) as i:
                for off in (1, 2):
                    turn(Batch(i, off))
            turn(Batch(0, B - 3))
            turn(Batch(0, B - 2), two=False)
            turn(Batch(0, B - 1), one=False, two=False)
            attn_high(Batch(0, B - 1))

            act.wait_ge(mom2_ready, NT)
            act.activation(std[:, 0:NT], moments[:, 0:NT, 1], ACT.Sqrt, bias=eps_c[:, :]).then_inc(std2_ready, 1)
            for n in range(NT):
                act.wait_ge(ft_done, n + 1)
                act.copy(fh[:, :, n * P:(n + 1) * P],
                         ps[:, n % 3, 0:KD * P].rearrange("p (k n) -> p k n", k=KD)).then_inc(fh_ready, 1)
            act.wait_ge(gate_step, 3)
            act.activation(gates[2][:, :, :], gates[1][:, :, :], ACT.Exp).then_inc(gate_exp, 1)

            def silu(s, par):
                act.wait_ge(h_done, s + 1)
                if not isinstance(s, int) or s >= 2:
                    act.wait_ge(hl_ready, s - 1)
                    act.wait_ge(y_done, s - 1)
                src = ps[:, 2 * par:2 * par + 2, :].rearrange("p a (b n) -> p (a b) n", b=2)
                act.activation(hh[par][:, :, :], src, ACT.Silu).then_inc(hh_ready, 1)
                act.activation(hf[par][:, :, :], src, ACT.Silu).then_inc(hf_ready, 1)

            silu(0, 0)
            silu(1, 1)
            with act.Fori(1, STEPS // 2) as i:
                silu(2 * i, 0)
                silu(2 * i + 1, 1)

        @block.vector
        def _(dve):
            def attn_weight_low(n):
                dve.wait_ge(wh_ready, n + 1)
                dve.tensor_tensor(wl[:, n, :, :], wraw[n], wh[:, n, :, :].bitcast(F32), ALU.subtract)\
                    .then_inc(wl_ready, 1)

            def masks(b):
                dve.wait_ge(ctx_in[b.par], 48 * (b.turn + 1))
                if not (isinstance(b.n, int) and b.n < 2):
                    dve.wait_ge(k_stacked[b.par], 64 * b.turn)
                else:
                    dve.wait_ge(zeros_set, 1)
                dve.tensor_scalar(keep[b.par][:, :], m_raw[b.par][:, :], 0.0, None, ALU.not_equal)\
                    .then_inc(keep_ready, 1)
                dve.wait_ge(keep_ready, b.n + 1)
                dve.tensor_scalar(m_row[b.par][:, :], keep[b.par][0:2, :], mask_c[:, 0:1], mask_c[:, 1:2],
                                  ALU.mult, ALU.add).then_inc(mrow_ready, 1)

            def keys(b):
                for t in range(KD):
                    dve.wait_ge(kproj_done, 2 * b.n + t + 1)
                    if t == 0 and not (isinstance(b.n, int) and b.n < 1):
                        dve.wait_ge(kl_ready, b.n)
                    dve.scalar_tensor_tensor(out=kf[:, t, :], in0=ps[:, BK_KV + t, 0:CP], scalar=bk_c[:, t:t + 1],
                                             in1=keep[b.par][:, :], op0=ALU.add, op1=ALU.mult)\
                        .then_inc(kf_ready, 1)

            def values(b):
                for k in range(KT):
                    if k != 1:
                        dve.wait_ge(vproj_done, 2 * b.n + (1 if k == 0 else 2))
                    if k == 0 and not (isinstance(b.n, int) and b.n < 2):
                        dve.wait_ge(pv_done, QUADS * (b.n - 1))
                    src = ps[0:CT, BK_KV + k // 2, D * (k % 2):D * (k % 2) + D]
                    dve.tensor_tensor(v1[b.par][:, k, :, 0:DK], src.rearrange("p (h d) -> p h d", h=H),
                                      bv_b[0:CT, :].rearrange("p (h d) -> p h d", h=H), ALU.add)\
                        .then_inc(v_ready, 1)

            def attn_low(b):
                dve.wait_ge(th_ready, b.n + 1)
                col = bass.ds(S * b.n, S)
                dve.tensor_tensor(tl[:, :, col], ps[:, BK_OUT, 0:KD * S].rearrange("p (k n) -> p k n", k=KD),
                                  th[:, :, col].bitcast(F32), ALU.subtract).then_inc(tl_ready, 1)

            def max_rows(b):
                dve.wait_ge(maxt_done, b.n + 1)
                if not (isinstance(b.n, int) and b.n < 1):
                    before = b.after(-1)
                    dve.wait_ge(mx_stacked[before.par], 32 * (before.turn + 1))
                dve.tensor_copy(mx_h[:, :], ps[0:H, BK_MAX, 0:S]).then_inc(mx_ready, 1)
                dve.wait_ge(mx_ready, 2 * b.n + 1)
                dve.tensor_tensor(mx_l[:, :], ps[0:H, BK_MAX, 0:S], mx_h[:, :].bitcast(F32), ALU.subtract)\
                    .then_inc(mx_ready, 1)

            def maxima(b):
                for h in range(H):
                    dve.wait_ge(smax_done, H * b.n + h + 1)
                    if h == 0 and not (isinstance(b.n, int) and b.n < 1):
                        dve.wait_ge(maxt_done, b.n)
                    dve.tensor_reduce(neg_max[:, h:h + 1], ps[0:S, BK_MAX + h % 2, 0:CP], AX.X, ALU.max,
                                      negate=True).then_inc(max_read, 1)

            def normalise(b):
                dve.wait_ge(pv_done, QUADS * (b.n + 1))
                o = ps[0:S, BK_OUT, 0:H * (DK + 1)].rearrange("p (h d) -> p h d", h=H)
                dve.reciprocal(rsum[:, :], o[:, :, DK]).then_inc(rsum_ready, 1)
                dve.wait_ge(rsum_ready, b.n + 1)
                if not (isinstance(b.n, int) and b.n < 1):
                    dve.wait_ge(at_done, b.n)
                dve.tensor_tensor(an[:, :].rearrange("p (h d) -> p h d", h=H), o[:, :, 0:DK],
                                  rsum[:, :].rearrange("p (h a) -> p h a", a=1).to_broadcast([S, H, DK]),
                                  ALU.mult).then_inc(an_ready, 1)

            first = Batch(0, 0)
            dve.memset(mask_c[:, 0:1], -NEG_LO)
            dve.memset(mask_c[:, 1:2], NEG_LO).then_inc(const_set, 1)
            dve.wait_ge(const_set, 1)
            dve.memset(mask_c[0:1, 0:1], -NEG_HI)
            dve.memset(mask_c[0:1, 1:2], NEG_HI).then_inc(const_set, 1)
            dve.wait_ge(const_set, 2)
            attn_weight_low(0)
            masks(first)
            attn_weight_low(1)
            dve.wait_ge(xr_in, 16)
            for b in range(B):
                dve.bn_stats(stats[0:S, b, :], xr[:, b, :]).then_inc(stats_ready, 1)
            for b in range(B):
                dve.wait_ge(stats_ready, b + 1)
                dve.bn_aggr(moments[0:S, b, :], stats[0:S, b, :]).then_inc(mom_ready, 1)
            dve.wait_ge(bias_in, 64)
            keys(first)
            values(first)
            dve.wait_ge(std_ready, 1)
            dve.reciprocal(rstd[0:S, :], std[0:S, :]).then_inc(rstd_ready, 1)
            dve.wait_ge(rstd_ready, 1)
            for b in range(B):
                dve.tensor_scalar(xr[:, b, :], xr[:, b, :], moments[0:S, b, 0:1], rstd[0:S, b:b + 1],
                                  ALU.subtract, ALU.mult).then_inc(xn_ready, 1)
            masks(first.after(1))
            attn_weight_low(2)
            attn_weight_low(3)
            dve.wait_ge(rw_ready, 1)
            dve.tensor_tensor(rwl[:, :, :], rw_raw[:, :, :], rwh[:, :, :].bitcast(F32), ALU.subtract)\
                .then_inc(rw_ready, 1)

            def x_low(g):
                dve.wait_ge(xh_ready, g + 1)
                dve.tensor_tensor(xl[g % 2][:, :, :], ps[:, 0:2, 0:SG], xh[g % 2][:, :, :].bitcast(F32),
                                  ALU.subtract).then_inc(xl_ready, 1)

            def queries(g):
                for t in range(KD):
                    dve.wait_ge(qproj_done, 2 * g + t + 1)
                    if g and t == 0:
                        dve.wait_ge(ql_ready, g)
                    dve.tensor_scalar(qf[:, t, :], ps[:, (2, BK_OUT)[t], 0:SG], bq_c[:, t:t + 1], DK ** -0.5,
                                      ALU.add, ALU.mult).then_inc(qf_ready, 1)
                dve.wait_ge(qh_ready, g + 1)
                dve.tensor_tensor(ql[0][:, :, :], qf[:, :, :], qh[0][:, :, :].bitcast(F32), ALU.subtract)\
                    .then_inc(ql_ready, 1)

            x_low(0)
            for g in range(NG):
                if g + 1 < NG:
                    x_low(g + 1)
                queries(g)
            maxima(first)

            def turn(b, one=True, two=True, prev=True):
                max_rows(b)
                if one:
                    keys(b.after(1))
                if prev:
                    attn_low(b.after(-1))
                if one:
                    values(b.after(1))
                if two:
                    masks(b.after(2))
                if one:
                    maxima(b.after(1))
                normalise(b)

            turn(first, prev=False)
            with dve.Fori(0, (B - 4) // 2) as i:
                for off in (1, 2):
                    turn(Batch(i, off))
            turn(Batch(0, B - 3))
            turn(Batch(0, B - 2), two=False)
            turn(Batch(0, B - 1), one=False, two=False)
            attn_low(Batch(0, B - 1))

            dve.wait_ge(xb_ready, 1)
            for n in range(NT):
                dve.wait_ge(oproj_done, n + 1)
                dve.tensor_tensor(x2[:, n, :], ps[:, 3 + n % 3, 0:D], x2[:, n, :], ALU.add).then_inc(x2_added, 1)
                dve.wait_ge(x2_added, n + 1)
                dve.bn_stats(stats[:, n, :], x2[:, n, :]).then_inc(st2_ready, 1)
                dve.wait_ge(st2_ready, n + 1)
                dve.bn_aggr(moments[:, n, :], stats[:, n, :]).then_inc(mom2_ready, 1)
            dve.wait_ge(std2_ready, 1)
            dve.reciprocal(rstd[:, 0:NT], std[:, 0:NT]).then_inc(rstd2_ready, 1)
            dve.wait_ge(rstd2_ready, 1)

            def flat_low(n):
                dve.wait_ge(fh_ready, n + 1)
                col = slice(n * P, (n + 1) * P)
                dve.tensor_tensor(fl[:, :, col], ps[:, n % 3, 0:KD * P].rearrange("p (k n) -> p k n", k=KD),
                                  fh[:, :, col].bitcast(F32), ALU.subtract).then_inc(fl_ready, 1)

            for n in range(NT):
                dve.tensor_scalar(xn2[:, n, :], x2[:, n, :], moments[:, n, 0:1], rstd[:, n:n + 1],
                                  ALU.subtract, ALU.mult).then_inc(xn2_ready, 1)
                if n >= 2:
                    flat_low(n - 2)
            flat_low(NT - 2)
            flat_low(NT - 1)

            logits, shifted, expd, picked, rest, t0, t1, pos = gates
            c0, c1, c2, c3 = gcol
            n_steps = [0]

            def step(ins):
                n_steps[0] += 1
                ins.then_inc(gate_step, 1)
                dve.wait_ge(gate_step, n_steps[0])

            def wide(col):
                return col[:, :].rearrange("p (n a) -> p n a", a=1).to_broadcast([P, NT, E])

            dve.wait_ge(route_done, NT)
            step(dve.tensor_copy(logits[:, :, :], ps[:, 6, 0:NT * E].rearrange("p (n e) -> p n e", n=NT)))
            step(dve.tensor_reduce(c0[:, :], logits[:, :, :], AX.X, ALU.max))
            step(dve.tensor_tensor(shifted[:, :, :], logits[:, :, :], wide(c0), ALU.subtract))
            for e in range(E):
                last = dve.memset(pos[:, :, e:e + 1], float(E - e))
            step(last)

            def first_of(src, col, dst):
                step(dve.tensor_tensor(t0[:, :, :], src, wide(col), ALU.is_equal))
                step(dve.tensor_tensor(t1[:, :, :], t0[:, :, :], pos[:, :, :], ALU.mult))
                step(dve.tensor_reduce(c1[:, :], t1[:, :, :], AX.X, ALU.max))
                step(dve.tensor_tensor(dst, t1[:, :, :], wide(c1), ALU.is_equal))

            first_of(logits[:, :, :], c0, picked[:, :, :])
            step(dve.scalar_tensor_tensor(out=rest[:, :, :], in0=picked[:, :, :], scalar=-3.0e38,
                                          in1=logits[:, :, :], op0=ALU.mult, op1=ALU.add))
            step(dve.tensor_reduce(c2[:, :], rest[:, :, :], AX.X, ALU.max))
            first_of(rest[:, :, :], c2, cw[:, :, :])
            step(dve.tensor_tensor(picked[:, :, :], picked[:, :, :], cw[:, :, :], ALU.add))
            dve.wait_ge(gate_exp, 1)
            step(dve.tensor_reduce(c0[:, :], expd[:, :, :], AX.X, ALU.add))
            step(dve.reciprocal(c1[:, :], c0[:, :]))
            step(dve.tensor_tensor(t0[:, :, :], expd[:, :, :], wide(c1), ALU.mult))
            step(dve.tensor_tensor(t1[:, :, :], t0[:, :, :], picked[:, :, :], ALU.mult))
            step(dve.tensor_reduce(c2[:, :], t1[:, :, :], AX.X, ALU.add))
            step(dve.tensor_scalar(c3[:, :], c2[:, :], GATE_EPS, None, ALU.max))
            step(dve.reciprocal(c0[:, :], c3[:, :]))
            step(dve.tensor_tensor(cw[:, :, :], t1[:, :, :], wide(c0), ALU.mult))

            def h_low(s, par):
                dve.wait_ge(hh_ready, s + 1)
                dve.wait_ge(hf_ready, s + 1)
                dve.tensor_tensor(hl[par][:, :, :], hf[par][:, :, :], hh[par][:, :, :].bitcast(F32),
                                  ALU.subtract).then_inc(hl_ready, 1)

            def add_y(s, e, g, par):
                dve.wait_ge(y_done, s + 1)
                dve.wait_ge(x2_added, 2 * (s + 1))
                for a in range(2):
                    n = 2 * g + a
                    dve.scalar_tensor_tensor(out=x2[:, n, :], in0=ps[:, 4 + par, D * a:D * a + D],
                                             scalar=cw[:, n, bass.ds(e, 1)], in1=x2[:, n, :],
                                             op0=ALU.mult, op1=ALU.add).then_inc(x2_added, 1)

            h_low(0, 0)
            with dve.Fori(0, E // 2 - 1) as i:
                for j in range(2 * NTG):
                    s = 2 * NTG * i + j
                    h_low(s + 1, (j + 1) % 2)
                    add_y(s, 2 * i + j // NTG, j % NTG, j % 2)
            for j in range(2 * NTG):
                s = STEPS - 2 * NTG + j
                if s + 1 < STEPS:
                    h_low(s + 1, (j + 1) % 2)
                add_y(s, E - 2 + j // NTG, j % NTG, j % 2)

        @block.tensor
        def _(pe):
            def product(o, terms):
                for n, (lhs, rhs) in enumerate(terms):
                    last = pe.matmul(o, lhs, rhs, start=n == 0, stop=n == len(terms) - 1)
                return last

            def project_keys(b):
                pe.wait_ge(ch_ready, b.n + 1)
                pe.wait_ge(cl_ready, b.n + 1)
                if not (isinstance(b.n, int) and b.n < 1):
                    pe.wait_ge(v_ready, KT * b.n)
                for t in range(KD):
                    m = slice(t * P, (t + 1) * P)
                    product(ps[:, BK_KV + t, 0:CP],
                            [(w[:, 0, k, m], c[b.par][:, k, :]) for k in range(KD)
                             for w, c in ((wh, ch), (wl, ch), (wh, cl))]).then_inc(kproj_done, 1)

            def project_values(b):
                for k3 in range(KT):
                    if k3 != 1:
                        pe.wait_ge(kf_ready, 2 * b.n + 1 + (k3 == 2))
                    m = slice(k3 * CT, (k3 + 1) * CT)
                    last = product(ps[0:CT, BK_KV + k3 // 2, D * (k3 % 2):D * (k3 % 2) + D],
                                   [(c[b.par][:, k, m], w[:, 1, k, :]) for k in range(KD)
                                    for w, c in ((wh, ch), (wh, cl), (wl, ch))])
                    if k3 != 0:
                        last.then_inc(vproj_done, 1)

            def head_scores(b, h):
                if h == 0:
                    pe.wait_ge(k_stacked[b.par], 64 * (b.turn + 1))
                    pe.wait_ge(q_stacked[b.par], 96 * (b.turn + 1))
                    if not (isinstance(b.n, int) and b.n < 1):
                        pe.wait_ge(mx_ready, 2 * b.n)
                if not (isinstance(b.n, int) and b.n < 1 and h < 2):
                    pe.wait_ge(max_read, H * b.n + h - 1)
                pe.matmul(ps[0:S, BK_MAX + h % 2, 0:CP], qs[b.par][0:R_MAX, h // 2, S * (h % 2):S * (h % 2) + S],
                          ks[b.par][0:R_MAX, h // 2, :], start=True, stop=True).then_inc(smax_done, 1)

            def max_transpose(b):
                pe.wait_ge(max_read, H * (b.n + 1))
                pe.transpose(ps[0:H, BK_MAX, 0:S], neg_max[:, :], ident[0:S, 0:S]).then_inc(maxt_done, 1)

            def quad_scores(b, j):
                if j == 0:
                    pe.wait_ge(mx_stacked[b.par], 32 * (b.turn + 1))
                if not (isinstance(b.n, int) and b.n < 1 and j < 1):
                    pe.wait_ge(p_ready, QUADS * b.n + j)
                for k3 in range(KT):
                    for q in range(2):
                        last = pe.matmul(ps[0:CT, BK_ST + k3, 2 * S * q:2 * S * (q + 1)],
                                         ks[b.par][0:ROWS, 2 * j + q, k3 * CT:(k3 + 1) * CT],
                                         qs[b.par][0:ROWS, 2 * j + q, :], start=True, stop=True)
                last.then_inc(st_done, 1)

            def head_output(b, j, q):
                h = 4 * j + q
                if q == 0:
                    pe.wait_ge(p_ready, QUADS * b.n + j + 1)
                if h == 0:
                    pe.wait_ge(v_ready, KT * (b.n + 1))
                    if not (isinstance(b.n, int) and b.n < 1):
                        pe.wait_ge(tl_ready, b.n)
                for k3 in range(KT):
                    last = pe.matmul(ps[0:S, BK_OUT, (DK + 1) * h:(DK + 1) * (h + 1)],
                                     pr[j % 2][:, k3, S * q:S * (q + 1)], v1[b.par][:, k3, h, :],
                                     start=k3 == 0, stop=k3 == KT - 1)
                if q == 3:
                    last.then_inc(pv_done, 1)

            def attn_transpose(b):
                pe.wait_ge(an_ready, b.n + 1)
                for k in range(KD):
                    last = pe.transpose(ps[:, BK_OUT, S * k:S * (k + 1)], an[:, k * P:(k + 1) * P], ident[0:S, 0:S])
                last.then_inc(at_done, 1)

            def turn(b, one=True, prev=True):
                max_transpose(b)
                if one:
                    project_keys(b.after(1))
                if prev:
                    attn_transpose(b.after(-1))
                if one:
                    project_values(b.after(1))
                quad_scores(b, 0)
                n = 0
                for j in range(QUADS):
                    if j + 1 < QUADS:
                        quad_scores(b, j + 1)
                    for q in range(4):
                        head_output(b, j, q)
                        if one and j >= 1:
                            for _ in range(1 + (n % 3 == 2)):
                                head_scores(b.after(1), n + n // 3 + (_ if n % 3 == 2 else 0))
                            n += 1

            first = Batch(0, 0)
            pe.wait_ge(wl_ready, 1)
            pe.wait_ge(filled, 8)
            project_keys(first)
            pe.wait_ge(wl_ready, 2)
            project_values(first)

            def x_transpose(g):
                pe.wait_ge(xn_ready, GB * (g + 1))
                if g == 0:
                    pe.wait_ge(ident_set, 2)
                else:
                    pe.wait_ge(xl_ready, g)
                for k in range(KD):
                    for b in range(GB):
                        last = pe.transpose(ps[:, k, S * b:S * (b + 1)], xr[:, GB * g + b, k * P:(k + 1) * P],
                                            ident[0:S, 0:S])
                last.then_inc(xt_done, 1)

            def project_queries(g):
                pe.wait_ge(wl_ready, 3)
                pe.wait_ge(xl_ready, g + 1)
                for t in range(KD):
                    if g >= 1:
                        pe.wait_ge(qf_ready, 2 * g - 1 + t)
                    m = slice(t * P, (t + 1) * P)
                    product(ps[:, (2, BK_OUT)[t], 0:SG],
                            [(w[:, 2, k, m], x[g % 2][:, k, :]) for k in range(KD)
                             for w, x in ((wh, xh), (wl, xh), (wh, xl))]).then_inc(qproj_done, 1)

            x_transpose(0)
            for g in range(NG):
                if g + 1 < NG:
                    x_transpose(g + 1)
                project_queries(g)
            for h in range(H):
                head_scores(first, h)
            turn(first, prev=False)
            with pe.Fori(0, (B - 4) // 2) as i:
                for off in (1, 2):
                    turn(Batch(i, off))
            turn(Batch(0, B - 3))
            turn(Batch(0, B - 2))
            turn(Batch(0, B - 1), one=False)
            attn_transpose(Batch(0, B - 1))

            pe.wait_ge(wl_ready, 4)
            pe.wait_ge(th_ready, B)
            pe.wait_ge(tl_ready, B)
            for n in range(NT):
                if n == 0:
                    pe.wait_ge(mx_ready, 2 * B)
                if n >= 3:
                    pe.wait_ge(x2_added, n - 2)
                m = slice(n * P, (n + 1) * P)
                product(ps[:, 3 + n % 3, 0:D],
                        [(a[:, k, m], w[:, 3, k, :]) for k in range(KD)
                         for a, w in ((th, wh), (th, wl), (tl, wh))]).then_inc(oproj_done, 1)

            def flat_transpose(n):
                pe.wait_ge(xn2_ready, n + 1)
                if n == 0:
                    pe.wait_ge(p_ready, QUADS * B)
                if n >= 3:
                    pe.wait_ge(fl_ready, n - 2)
                for k in range(KD):
                    last = pe.transpose(ps[:, n % 3, k * P:(k + 1) * P], xn2[:, n, k * P:(k + 1) * P], ident[:, :])
                last.then_inc(ft_done, 1)

            def route(n):
                pe.wait_ge(fl_ready, n + 1)
                if n == 0:
                    pe.wait_ge(rw_ready, 2)
                m = slice(n * P, (n + 1) * P)
                product(ps[:, 6, E * n:E * (n + 1)],
                        [(f[:, k, m], w[:, k, :]) for k in range(KD)
                         for f, w in ((fh, rwh), (fh, rwl), (fl, rwh))]).then_inc(route_done, 1)

            for n in range(NT):
                flat_transpose(n)
                if n >= 2:
                    route(n - 2)
            route(NT - 2)
            route(NT - 1)

            def hidden(s, g, par, wpar, e):
                if g == 0:
                    pe.wait_ge(ew_ready, 4 * (e + 1))
                if not isinstance(s, int) or s >= 2:
                    pe.wait_ge(hf_ready, s - 1)
                elif s == 0:
                    pe.wait_ge(x2_added, NT)
                m = slice(g * TG, (g + 1) * TG)
                for f in range(KF):
                    c = slice(f * P, (f + 1) * P)
                    last = product(ps[:, 2 * par + f // 2, TG * (f % 2):TG * (f % 2 + 1)],
                                   [(w[wpar][:, k, c], x[:, k, m]) for k in range(KD)
                                    for w, x in ((w1h, fh), (w1l, fh), (w1h, fl))])
                last.then_inc(h_done, 1)

            def expert_out(s, par, wpar):
                pe.wait_ge(hl_ready, s + 1)
                pe.wait_ge(x2_added, NT + 2 * s - 2 if not isinstance(s, int) or s >= 2 else NT)
                for a in range(2):
                    m = slice(a * P, (a + 1) * P)
                    last = product(ps[:, 4 + par, D * a:D * (a + 1)],
                                   [(x[par][:, f, m], w[wpar][:, f, :]) for f in range(KF)
                                    for x, w in ((hh, w2h), (hh, w2l), (hl, w2h))])
                last.then_inc(y_done, 1)

            hidden(0, 0, 0, 0, 0)
            with pe.Fori(0, E // 2 - 1) as i:
                for j in range(2 * NTG):
                    s, nxt = 2 * NTG * i + j, j + 1
                    hidden(s + 1, nxt % NTG, nxt % 2, (nxt // NTG) % 2, 2 * i + nxt // NTG)
                    expert_out(s, j % 2, j // NTG)
            for j in range(2 * NTG):
                s, nxt = STEPS - 2 * NTG + j, j + 1
                if s + 1 < STEPS:
                    hidden(s + 1, nxt % NTG, nxt % 2, nxt // NTG, E - 2 + nxt // NTG)
                expert_out(s, j % 2, j // NTG)


def kernel(x, ctx_1024, mask_BxS2_ik0, L0_xattn_Wq, L0_xattn_bq, L0_xattn_Wk, L0_xattn_bk, L0_xattn_Wv,
           L0_xattn_bv, L0_xattn_Wo, L0_xattn_bo, L0_ffn_router_w, L0_ffn_w1, L0_ffn_w2):
    import numpy as np
    import concourse.bacc as bacc
    from concourse.bass_utils import run_bass_kernel_spmd

    def halves(w):
        return np.ascontiguousarray(np.asarray(w)).reshape(KD, P, -1)

    x = np.asarray(x)
    arrays = {
        "x_rows": x,
        "x_tiles": x.reshape(NT, P, D),
        "ctx_t": np.ascontiguousarray(np.asarray(ctx_1024).transpose(2, 0, 1)).reshape(KD, P, B, C),
        "mask": np.asarray(mask_BxS2_ik0),
        "wq_t": halves(np.asarray(L0_xattn_Wq).T),
        "wk_t": halves(np.asarray(L0_xattn_Wk).T),
        "wv_t": halves(np.asarray(L0_xattn_Wv).T),
        "wo_t": halves(np.asarray(L0_xattn_Wo).T),
        "bq": np.ascontiguousarray(np.asarray(L0_xattn_bq).reshape(KD, P).T),
        "bk": np.ascontiguousarray(np.asarray(L0_xattn_bk).reshape(KD, P).T),
        "bv": np.asarray(L0_xattn_bv).reshape(1, D),
        "bo": np.asarray(L0_xattn_bo).reshape(1, D),
        "router_w": halves(L0_ffn_router_w),
        "w1": np.ascontiguousarray(np.asarray(L0_ffn_w1)).reshape(E, KD, P, F),
        "w2": np.ascontiguousarray(np.asarray(L0_ffn_w2)).reshape(E, KF, P, D),
    }
    nc = bacc.Bacc("TRN2", target_bir_lowering=False, num_devices=1)
    args = [nc.dram_tensor(n, a.shape, mybir.dt.from_np(a.dtype), kind="ExternalInput").ap()
            for n, a in arrays.items()]
    args.append(nc.dram_tensor("out", (NT, P, D), F32, kind="ExternalOutput").ap())
    xattn_moe_kernel(nc, *args)
    r = run_bass_kernel_spmd(nc, [arrays], core_ids=[0])
    return np.asarray(r.results[0]["out"]).reshape(B, S, D)
```

```python
from contextlib import ExitStack

import concourse.bass as bass
from concourse import mybir

F32 = mybir.dt.float32
F32R = mybir.dt.float32r
I32 = mybir.dt.int32
ALU = mybir.AluOpType
ACT = mybir.ActivationFunctionType
AX = mybir.AxisListType

P = 128
B, S, D = 16, 112, 256
C = 375
CP = C + 1
H, DK = 16, 16
E, F = 8, 512
KD = D // P
KF = F // P
KT = 3
CT = C // KT
PAIRS = H // 2
QUADS = H // 4
T = B * S
NT = T // P
GB = 4
NG = B // GB
SG = GB * S
TG = 2 * P
NTG = T // TG
STEPS = E * NTG
NEG = -1.0e9
NEG_HI = -1000079360.0
NEG_LO = NEG - NEG_HI
LN_EPS = 1e-5
GATE_EPS = 1e-9

PARTS = 3
HALF = H // 2
R_MASK, R_MAX, ROWS = 96, 98, 100

A1 = 64
VM = A1 + 2 * DK + 1
VW = VM + 1
OW = 2 * DK + 1
MAGIC = 0x5f3759df

BK_ST, BK_MAX, BK_KV, BK_OUT = 0, 3, 5, 7
BK_AT = BK_MAX + 1
BK_Y, BK_A, BK_T = 4, 6, 7
N_FILLS = 10
LOOPS = (B - 6) // 2


class Batch:

    def __init__(self, i, off):
        self.i, self.off = i, off
        self.par, self.turn, self.n = off % 2, i + off // 2, 2 * i + off

    def after(self, k):
        return Batch(self.i, self.off + k)


def xattn_moe_kernel(nc, x_rows, x_tiles, ctx_t, mask, wq_t, wk_t, wv_t, wo_t, bq, bk, bv, bo,
                     router_w, w1, w2, out):
    ctx = ExitStack()
    with ctx:
        def sem(name):
            return ctx.enter_context(nc.semaphore(name))

        base = (nc.sbuf_base + 63) // 64 * 64
        cursor = {"at": base, "top": base}

        def sb(name, shape, dt=F32):
            size = 4
            for n in shape[1:]:
                size *= n
            off = cursor["at"]
            cursor["at"] += (size + 63) // 64 * 64
            cursor["top"] = max(cursor["top"], cursor["at"])
            return nc.alloc_sbuf_tensor_at(name, shape, dt, offset=off)

        ident = sb("ident", [P, P])
        th = sb("attn_t_hi", [P, KD, T], F32R)
        tl = sb("attn_t_lo", [P, KD, T], F32R)
        wh = sb("attn_w_hi", [P, 4, KD, D], F32R)
        wl = sb("attn_w_lo", [P, 4, KD, D], F32R)
        rw_raw = sb("router_raw", [P, KD, E])
        rwh = sb("router_hi", [P, KD, E], F32R)
        rwl = sb("router_lo", [P, KD, E], F32R)
        bv_b = sb("bv_b", [P, D])
        bo_b = sb("bo_b", [P, D])
        bq_c = sb("bq_c", [P, KD])
        bk_c = sb("bk_c", [P, KD])
        mask_c = sb("mask_c", [2, 2])
        stats = sb("stats", [P, B, 6])
        moments = sb("moments", [P, B, 2])
        std = sb("std", [P, B])
        rstd = sb("rstd", [P, B])
        pos = sb("gate_pos", [P, 2, E])
        eps_c = sb("eps_c", [P, 1])
        w1_raw = sb("w1_raw", [P, KD, F])
        w2_raw = sb("w2_raw", [P, KF, D])
        wraw = [w1_raw[:, 0:2, 0:256], w1_raw[:, 0:2, 256:512], w2_raw[:, 0:2, :], w2_raw[:, 2:4, :]]

        shared = cursor["at"]
        xh = [sb(f"x_t_hi{p}", [P, KD, SG], F32R) for p in range(2)]
        xl = [sb(f"x_t_lo{p}", [P, KD, SG], F32R) for p in range(2)]
        q_end = cursor["at"]

        def expert_buffers(p):
            return (sb(f"w1_hi{p}", [P, KD, F], F32R), sb(f"w1_lo{p}", [P, KD, F], F32R),
                    sb(f"w2_hi{p}", [P, KF, D], F32R), sb(f"w2_lo{p}", [P, KF, D], F32R))

        cursor["at"] = shared
        expert_even = expert_buffers(0)
        cursor["at"] = max(q_end, cursor["at"])

        attn_start = cursor["at"]
        c_raw = [sb(f"ctx_raw{p}", [P, KD, CP]) for p in range(2)]
        ch = [sb(f"ctx_hi{p}", [P, KD, CP], F32R) for p in range(2)]
        cl = [sb(f"ctx_lo{p}", [P, KD, CP], F32R) for p in range(2)]
        m_raw = [sb(f"mask_raw{p}", [P, CP], I32) for p in range(2)]
        keep = [sb(f"keep{p}", [P, CP]) for p in range(2)]
        m_row = [sb(f"mask_row{p}", [2, CP], F32R) for p in range(2)]
        kf = sb("k_f32", [P, KD, CP])
        kh = sb("k_hi", [P, KD, CP], F32R)
        kl = sb("k_lo", [P, KD, CP], F32R)
        ks = [sb(f"k_stack{p}", [P, PAIRS, CP], F32R) for p in range(2)]
        qs = [sb(f"q_stack{p}", [P, PAIRS, 2 * S], F32R) for p in range(2)]
        vf = sb("v_f32", [CT, KT, D])
        vs = [sb(f"v_stack{p}", [CT, KT, PAIRS, VW], F32R) for p in range(2)]
        q_hl_at = cursor["at"]
        pf = [sb(f"probs_f32{p}", [CT, KT, 4 * S]) for p in range(2)]
        ph = [sb(f"probs_hi{p}", [CT, KT, 4 * S], F32R) for p in range(2)]
        pl = [sb(f"probs_lo{p}", [CT, KT, 4 * S], F32R) for p in range(2)]
        ot_at = cursor["at"]
        ot = [sb(f"out_t{n}", [VM, 4 * S]) for n in range(QUADS)]
        neg_max = sb("neg_max", [S, H])
        mx_h = sb("max_hi", [H, S], F32R)
        mx_l = sb("max_lo", [H, S], F32R)
        rsum = sb("rsum", [S, H])
        ah = sb("attn_rows", [S, D])
        al = sb("attn_rows_by_lo", [S, D])
        attn_end = cursor["at"]
        cursor["at"] = q_hl_at
        qh = [sb(f"q_hi{p}", [P, KD, SG], F32R) for p in range(2)]
        ql = [sb(f"q_lo{p}", [P, KD, SG], F32R) for p in range(2)]
        xr = sb("x_rows_sb", [S, B, D])
        assert cursor["at"] <= ot_at
        cursor["at"] = ot_at
        qf = sb("q_f32", [P, KD, SG])
        assert cursor["at"] <= ot_at + 2 * 4 * S * 4
        cursor["at"] = attn_start
        x2 = sb("x2", [P, NT, D])
        assert cursor["at"] <= attn_start + 6 * KD * CP * 4, "x2 lies where the context's parts were"
        hf = [sb(f"h_f32{p}", [P, KF, TG]) for p in range(2)]
        hh = [sb(f"h_hi{p}", [P, KF, TG], F32R) for p in range(2)]
        hl = [sb(f"h_lo{p}", [P, KF, TG], F32R) for p in range(2)]
        fh = sb("flat_t_hi", [P, KD, T], F32R)
        fl = sb("flat_t_lo", [P, KD, T], F32R)
        xn2 = [sb(f"xn2_{p}", [P, 2, D]) for p in range(2)]
        gates = [sb(f"gate{n}", [P, 2, E]) for n in range(7)]
        gcol = [sb(f"gate_col{n}", [P, 2]) for n in range(4)]
        nw = [sb(f"newton{n}", [P, 2]) for n in range(4)]
        st2 = sb("stats2", [P, 2, 6])
        mo2 = sb("moments2", [P, 2, 2])
        cw = sb("gate_weights", [P, NT, E])
        w1h, w1l, w2h, w2l = zip(expert_even, expert_buffers(1))
        assert cursor["top"] <= nc.sbuf_usable_end, (cursor, nc.sbuf_usable_end)

        ps = ctx.enter_context(nc.psum_tensor("ps", [P, 8, 512], F32))

        k_scratch = [nc.dram_tensor(f"k_scratch{p}", [KD, H // KD, PARTS, DK, CP], F32).ap() for p in range(2)]
        q_scratch = nc.dram_tensor("q_scratch", [KD, H // KD, PARTS, DK, T], F32).ap()

        aw_in = [sem(f"aw_in{n}") for n in range(4)]
        ctx_in = [sem(f"ctx_in{p}") for p in range(2)]
        k_written = [sem(f"k_written{p}") for p in range(2)]
        stacked = [[sem(f"stacked{p}_{f}") for f in range(2)] for p in range(2)]
        mx_stacked = [sem(f"mx_stacked{p}") for p in range(2)]
        q_written = [sem(f"q_written{p}") for p in range(2)]
        bias_in, xr_in, x2_in, rw_in, ew_in = (sem(n) for n in (
            "bias_in", "xr_in", "x2_in", "rw_in", "ew_in"))
        zeros_set, const_set, ident_set, filled = (sem(n) for n in (
            "zeros_set", "const_set", "ident_set", "filled"))
        wh_ready, wl_ready, rw_ready = (sem(n) for n in (
            "wh_ready", "wl_ready", "rw_ready"))
        ch_ready, cl_ready, keep_ready, mrow_ready = (sem(n) for n in (
            "ch_ready", "cl_ready", "keep_ready", "mrow_ready"))
        kproj_done, kf_ready, kh_ready, kl_ready = (sem(n) for n in (
            "kproj_done", "kf_ready", "kh_ready", "kl_ready"))
        vproj_done, vf_ready, vh_ready, vl_ready = (sem(n) for n in (
            "vproj_done", "vf_ready", "vh_ready", "vl_ready"))
        smax_done, max_read, maxt_done, mx_ready = (sem(n) for n in (
            "smax_done", "max_read", "maxt_done", "mx_ready"))
        st_done, pf_ready, ph_ready, pl_even, pl_odd, pv_done = (sem(n) for n in (
            "st_done", "pf_ready", "ph_ready", "pl_even", "pl_odd", "pv_done"))
        ot_ready, ott_done, rsum_ready, o_read, an_ready, at_done = (sem(n) for n in (
            "ot_ready", "ott_done", "rsum_ready", "o_read", "an_ready", "at_done"))
        th_ready, tl_ready = (sem(n) for n in (
            "th_ready", "tl_ready"))
        stats_ready, mom_ready, std_ready, rstd_ready, xn_ready = (sem(n) for n in (
            "stats_ready", "mom_ready", "std_ready", "rstd_ready", "xn_ready"))
        xt_done, xh_ready, xl_ready = (sem(n) for n in (
            "xt_done", "xh_ready", "xl_ready"))
        qproj_done, qf_ready, qh_ready, ql_ready = (sem(n) for n in (
            "qproj_done", "qf_ready", "qh_ready", "ql_ready"))
        xb_ready, oproj_done, resid_added, chain_step, xn2_ready = (sem(n) for n in (
            "xb_ready", "oproj_done", "resid_added", "chain_step", "xn2_ready"))
        ft_done, fh_ready, fl_ready, route_done = (sem(n) for n in (
            "ft_done", "fh_ready", "fl_ready", "route_done"))
        logits_read, shifted_ready, gate_exp = (sem(n) for n in (
            "logits_read", "shifted_ready", "gate_exp"))
        ew_ready, h_done, hf_ready, hh_ready, hl_ready = (sem(n) for n in (
            "ew_ready", "h_done", "hf_ready", "hh_ready", "hl_ready"))
        y_done, y_added, out_written = (sem(n) for n in (
            "y_done", "y_added", "out_written"))

        v_rows = vf[:, :, :].rearrange("p k (h a d) -> p (k h) a d", a=2, d=DK)

        def v_part(b, part):
            cols = vs[b.par][:, :, :, :].rearrange("p k h n -> p (k h) n")
            return cols[:, :, DK * part:DK * part + A1 + DK].rearrange(
                "p h (a d) -> p h a d", d=DK)[:, :, 0::A1 // DK, :]

        def group(t, g):
            return t[:, :, g * TG:(g + 1) * TG]

        block = ctx.enter_context(nc.Block())

        def early(b, n):
            return isinstance(b.n, int) and b.n < n

        def has(b):
            return not isinstance(b.n, int) or 0 <= b.n < B

        @block.sync
        def _(sp):
            def load_ctx(b):
                if not early(b, 2):
                    sp.wait_ge(ch_ready, b.n - 1)
                    sp.wait_ge(cl_ready, b.n - 1)
                    sp.wait_ge(keep_ready, b.n - 1)
                for k in range(KD):
                    sp.dma_start(c_raw[b.par][:, k, 0:C], ctx_t[k, :, bass.ds(b.n, 1), :]
                                 .rearrange("p a n -> p (a n)")).then_inc(ctx_in[b.par], 16)
                sp.dma_start(m_raw[b.par][:, 0:C], mask[bass.ds(b.n, 1), :].to_broadcast([P, C]))\
                    .then_inc(ctx_in[b.par], 16)

            def write_keys(b):
                sp.wait_ge(kh_ready, b.n + 1)
                sp.wait_ge(kl_ready, b.n + 1)
                for c, src in enumerate((kh, kh, kl)):
                    for t in range(KD):
                        sp.dma_start(k_scratch[b.par][t, :, c, :, :], src[:, t, :].bitcast(F32))\
                            .then_inc(k_written[b.par], 16)

            def stack_half(b, f):
                if not early(b, 2):
                    sp.wait_ge(st_done, QUADS * (b.n - 2) + 2 * (f + 1))
                sp.wait_ge(k_written[b.par], 96 * (b.turn + 1))
                sp.wait_ge(mrow_ready, b.n + 1)
                pairs = slice(f * PAIRS // 2, (f + 1) * PAIRS // 2)
                sp.dma_start(ks[b.par][0:R_MASK, pairs, :].bitcast(F32),
                             k_scratch[b.par][f].rearrange("(q a) c d n -> (a c d) q n", a=2))\
                    .then_inc(stacked[b.par][f], 16)
                for a in range(2):
                    sp.dma_start(qs[b.par][48 * a:48 * a + 48, pairs, S * a:S * a + S].bitcast(F32),
                                 q_scratch[f, :, :, :, bass.ds(S * b.n, S)]
                                 .rearrange("(q a) c d n -> a (c d) q n", a=2)[a])\
                        .then_inc(stacked[b.par][f], 16)
                sp.dma_start(ks[b.par][R_MASK:R_MASK + 2, pairs, :].bitcast(F32),
                             m_row[b.par][:, :].bitcast(F32).rearrange("p (a n) -> p a n", a=1)
                             .to_broadcast([2, PAIRS // 2, CP])).then_inc(stacked[b.par][f], 16)

            def stack_max(b):
                sp.wait_ge(mx_ready, 2 * (b.n + 1))
                for r, src in ((0, mx_h), (1, mx_l)):
                    sp.dma_start(qs[b.par][R_MAX + r:R_MAX + r + 1, :, :].bitcast(F32)
                                 .rearrange("p q (a n) -> p (q a) n", a=2),
                                 src[:, :].bitcast(F32)).then_inc(mx_stacked[b.par], 16)

            def turn(b):
                if has(b.after(4)):
                    load_ctx(b.after(4))
                if has(b.after(2)):
                    write_keys(b.after(2))
                    stack_half(b.after(2), 0)
                if has(b.after(1)):
                    stack_max(b.after(1))
                if has(b.after(2)):
                    stack_half(b.after(2), 1)

            first = Batch(0, 0)
            sp.dma_start(wraw[0], wk_t.rearrange("k p n -> p k n")).then_inc(aw_in[0], 16)
            sp.wait_ge(zeros_set, 1)
            load_ctx(first)
            sp.dma_start(xr[:, :, :], x_rows.rearrange("b s d -> s b d")).then_inc(xr_in, 16)
            sp.dma_start(wraw[1], wv_t.rearrange("k p n -> p k n")).then_inc(aw_in[1], 16)
            sp.dma_start(bk_c[:, :], bk).then_inc(bias_in, 16)
            sp.dma_start(bv_b[:, :], bv.to_broadcast([P, D])).then_inc(bias_in, 16)
            sp.dma_start(bq_c[:, :], bq).then_inc(bias_in, 16)
            load_ctx(first.after(1))
            sp.dma_start(wraw[2], wq_t.rearrange("k p n -> p k n")).then_inc(aw_in[2], 16)
            sp.dma_start(wraw[3], wo_t.rearrange("k p n -> p k n")).then_inc(aw_in[3], 16)
            sp.dma_start(bo_b[:, :], bo.to_broadcast([P, D])).then_inc(bias_in, 16)
            sp.dma_start(rw_raw[:, :, :], router_w.rearrange("k p n -> p k n")).then_inc(rw_in, 16)
            write_keys(first)
            load_ctx(first.after(2))
            write_keys(first.after(1))
            load_ctx(first.after(3))
            for g in range(NG):
                sp.wait_ge(qh_ready, g + 1)
                sp.wait_ge(ql_ready, g + 1)
                for c, src in enumerate((qh, ql, qh)):
                    for t in range(KD):
                        sp.dma_start(q_scratch[t, :, c, :, SG * g:SG * g + SG],
                                     src[g % 2][:, t, :].bitcast(F32)).then_inc(q_written[g % 2], 16)
            sp.wait_ge(filled, N_FILLS)
            for p in range(2):
                sp.wait_ge(q_written[p], 96 * NG // 2)
            for b in (first, first.after(1)):
                for f in range(2):
                    stack_half(b, f)
            stack_max(first)
            turn(first)
            turn(first.after(1))
            with sp.Fori(0, LOOPS) as i:
                for off in (2, 3):
                    turn(Batch(i, off))
            sp.wait_ge(wh_ready, 4)
            sp.wait_ge(wl_ready, 4)
            sp.dma_start(w1_raw[:, :, :], w1[0].rearrange("k p n -> p k n")).then_inc(ew_in, 16)
            sp.dma_start(w2_raw[:, :, :], w2[0].rearrange("k p n -> p k n")).then_inc(ew_in, 16)
            for b in range(2 + 2 * LOOPS, B):
                turn(Batch(0, b))

            def load_expert(e):
                sp.wait_ge(ew_ready, 4 * e)
                sp.dma_start(w1_raw[:, :, :], w1[bass.ds(e, 1), :, :, :].rearrange("a k p n -> p (a k) n"))\
                    .then_inc(ew_in, 16)
                sp.dma_start(w2_raw[:, :, :], w2[bass.ds(e, 1), :, :, :].rearrange("a k p n -> p (a k) n"))\
                    .then_inc(ew_in, 16)

            sp.wait_ge(vproj_done, 2 * B)
            sp.dma_start(x2[:, :, :], x_tiles.rearrange("n p d -> p n d")).then_inc(x2_in, 16)
            with sp.Fori(1, E) as e:
                load_expert(e)
            for g in range(NTG):
                sp.wait_ge(y_added, 2 * ((E - 1) * NTG + g + 1))
                sp.dma_start(out[2 * g:2 * g + 2].rearrange("n p d -> p n d"), x2[:, 2 * g:2 * g + 2, :])\
                    .then_inc(out_written, 16)
            sp.wait_ge(out_written, 16 * NTG)

        @block.gpsimd
        def _(pool):
            for p in range(2):
                pool.memset(c_raw[p][:, :, C:CP], 0.0)
                last = pool.memset(m_raw[p][:, C:CP], 0)
            last.then_inc(zeros_set, 1)
            pool.memset(eps_c[:, :], LN_EPS)
            pool.memset(ident[:, :], 0.0).then_inc(ident_set, 1)
            pool.wait_ge(ident_set, 1)
            pool.affine_select(out=ident[:, :], in_=ident[:, :], compare_op=ALU.not_equal, fill=1.0, base=0,
                               pattern=[[-1, P]], channel_multiplier=1).then_inc(ident_set, 1)
            pool.wait_ge(ident_set, 2)

            def ctx_low(b):
                pool.wait_ge(ch_ready, b.n + 1)
                pool.tensor_tensor(cl[b.par][:, :, :], c_raw[b.par][:, :, :], ch[b.par][:, :, :].bitcast(F32),
                                   ALU.subtract).then_inc(cl_ready, 1)

            def key_low(b):
                pool.wait_ge(kh_ready, b.n + 1)
                if not early(b, 1):
                    before = b.after(-1)
                    pool.wait_ge(k_written[before.par], 96 * (before.turn + 1))
                pool.tensor_tensor(kl[:, :, :], kf[:, :, :], kh[:, :, :].bitcast(F32), ALU.subtract)\
                    .then_inc(kl_ready, 1)

            def value_low(b):
                pool.wait_ge(vh_ready, b.n + 1)
                heads = [v_part(b, part) for part in range(2)]
                pool.tensor_tensor(heads[1], v_rows, heads[0].bitcast(F32), ALU.subtract).then_inc(vl_ready, 1)

            def probs_low(b, j):
                pool.wait_ge(ph_ready, QUADS * b.n + j + 1)
                pool.tensor_tensor(pl[j % 2][:, :, :], pf[j % 2][:, :, :], ph[j % 2][:, :, :].bitcast(F32),
                                   ALU.subtract).then_inc(pl_odd, 1)

            def add_parts(b):
                pool.wait_ge(o_read, 2 * (b.n + 1))
                pool.tensor_tensor(ah[:, :], ah[:, :], al[:, :], ALU.add).then_inc(an_ready, 1)

            first = Batch(0, 0)
            ctx_low(first)
            pool.wait_ge(cl_ready, 1)
            fills = [(vs[p][:, :, :, OW - 1::A1], 1.0) for p in range(2)]
            fills += [(vs[p][:, :, :, OW:A1], 0.0) for p in range(2)]
            fills += [(ks[p][R_MASK:ROWS, :, :], 1.0) for p in range(2)]
            fills += [(qs[p][0:R_MASK, :, :], 0.0) for p in range(2)]
            fills += [(qs[p][R_MASK:ROWS, :, :], 1.0) for p in range(2)]
            assert len(fills) == N_FILLS
            for n, (what, value) in enumerate(fills):
                if n == 2:
                    ctx_low(first.after(1))
                    pool.wait_ge(cl_ready, 2)
                if n == 4:
                    key_low(first)
                    value_low(first)
                    pool.wait_ge(kl_ready, 1)
                    pool.wait_ge(vl_ready, 1)
                pool.memset(what.bitcast(F32), value).then_inc(filled, 1)
                pool.wait_ge(filled, n + 1)
            key_low(first.after(1))
            ctx_low(first.after(2))

            def turn(b):
                if has(b.after(-1)):
                    probs_low(b.after(-1), 3)
                if has(b.after(2)):
                    key_low(b.after(2))
                if has(b.after(3)):
                    ctx_low(b.after(3))
                if has(b):
                    probs_low(b, 1)
                if has(b.after(-1)):
                    add_parts(b.after(-1))
                if has(b.after(1)):
                    value_low(b.after(1))

            def split_high(e, par):
                pool.wait_ge(ew_in, 32 * (e + 1))
                if e >= 2:
                    pool.wait_ge(y_done, NTG * (e - 1))
                pool.tensor_copy(w1h[par][:, :, :], w1_raw[:, :, :]).then_inc(ew_ready, 1)
                pool.tensor_copy(w2h[par][:, :, :], w2_raw[:, :, :]).then_inc(ew_ready, 1)

            def split_low(e, par):
                pool.wait_ge(ew_ready, 4 * e + 2)
                pool.tensor_tensor(w1l[par][:, :, :], w1_raw[:, :, :], w1h[par][:, :, :].bitcast(F32),
                                   ALU.subtract).then_inc(ew_ready, 1)
                pool.tensor_tensor(w2l[par][:, :, :], w2_raw[:, :, :], w2h[par][:, :, :].bitcast(F32),
                                   ALU.subtract).then_inc(ew_ready, 1)

            turn(first)
            turn(first.after(1))
            with pool.Fori(0, LOOPS) as i:
                for off in (2, 3):
                    turn(Batch(i, off))
            turn(Batch(0, B - 4))
            turn(Batch(0, B - 3))
            pool.wait_ge(ql_ready, NG)
            pool.wait_ge(qproj_done, 2 * NG)
            split_high(0, 0)
            turn(Batch(0, B - 2))
            split_low(0, 0)
            turn(Batch(0, B - 1))
            turn(Batch(0, B))
            pool.wait_ge(x2_in, 16)
            pool.wait_ge(bias_in, 64)
            for g in range(NTG):
                pair = slice(2 * g, 2 * g + 2)
                pool.tensor_tensor(x2[:, pair, :], x2[:, pair, :],
                                   bo_b[:, :].rearrange("p (a n) -> p a n", a=1).to_broadcast([P, 2, D]),
                                   ALU.add).then_inc(xb_ready, 1)
            pool.wait_ge(tl_ready, B)
            for e in range(1, E):
                split_high(e, e % 2)
                split_low(e, e % 2)

        @block.scalar
        def _(act):
            def attn_weight(n):
                act.wait_ge(aw_in[n], 16)
                act.copy(wh[:, n, :, :], wraw[n]).then_inc(wh_ready, 1)

            def ctx_high(b):
                act.wait_ge(ctx_in[b.par], 48 * (b.turn + 1))
                if early(b, 2):
                    act.wait_ge(zeros_set, 1)
                else:
                    act.wait_ge(vproj_done, 2 * (b.n - 1))
                act.copy(ch[b.par][:, :, :], c_raw[b.par][:, :, :]).then_inc(ch_ready, 1)

            def key_high(b):
                act.wait_ge(kf_ready, 2 * (b.n + 1))
                if not early(b, 1):
                    before = b.after(-1)
                    act.wait_ge(k_written[before.par], 96 * (before.turn + 1))
                act.copy(kh[:, :, :], kf[:, :, :]).then_inc(kh_ready, 1)

            def value_high(b):
                act.wait_ge(vf_ready, 2 * (b.n + 1))
                if not early(b, 2):
                    act.wait_ge(pv_done, QUADS * (b.n - 1))
                act.copy(v_part(b, 0), v_rows).then_inc(vh_ready, 1)

            def attn_high(b):
                act.wait_ge(at_done, b.n + 1)
                act.copy(th[:, :, bass.ds(S * b.n, S)],
                         ps[:, BK_AT, 0:KD * S].rearrange("p (k n) -> p k n", k=KD)).then_inc(th_ready, 1)

            def exps(b, j):
                act.wait_ge(st_done, QUADS * b.n + j + 1)
                again = not (early(b, 1) and j < 2)
                if again:
                    act.wait_ge((pl_even, pl_odd)[j % 2], 2 * b.n + j // 2)
                src = ps[0:CT, BK_ST:BK_ST + KT, 0:4 * S]
                act.activation(pf[j % 2][:, :, :], src, ACT.Exp).then_inc(pf_ready, 1)
                if again:
                    act.wait_ge(pv_done, QUADS * b.n + j - 1)
                act.activation(ph[j % 2][:, :, :], src, ACT.Exp).then_inc(ph_ready, 1)

            def out_copy(b, j):
                act.wait_ge(pv_done, QUADS * b.n + j + 1)
                if j == 0 and not early(b, 1):
                    act.wait_ge(ott_done, b.n)
                act.copy(ot[j][:, :], ps[0:VM, BK_OUT, 0:4 * S]).then_inc(ot_ready, 1)

            attn_weight(0)
            first = Batch(0, 0)
            ctx_high(first)
            attn_weight(1)
            ctx_high(first.after(1))
            attn_weight(2)
            act.wait_ge(mom_ready, B)
            act.wait_ge(ident_set, 1)
            act.activation(std[0:S, :], moments[0:S, :, 1], ACT.Sqrt, bias=eps_c[0:S, :]).then_inc(std_ready, 1)
            key_high(first)
            value_high(first)

            def x_high(g):
                act.wait_ge(xt_done, g + 1)
                if g >= 2:
                    act.wait_ge(qproj_done, 2 * (g - 1))
                act.copy(xh[g % 2][:, :, :], ps[:, 0:2, 0:SG]).then_inc(xh_ready, 1)

            def q_high(g):
                act.wait_ge(qf_ready, 2 * (g + 1))
                if g >= 2:
                    act.wait_ge(q_written[g % 2], 96)
                act.copy(qh[g % 2][:, :, :], qf[:, :, :]).then_inc(qh_ready, 1)

            x_high(0)
            key_high(first.after(1))
            for g in range(NG):
                if g + 1 < NG:
                    x_high(g + 1)
                q_high(g)
            attn_weight(3)
            act.wait_ge(rw_in, 16)
            act.copy(rwh[:, :, :], rw_raw[:, :, :]).then_inc(rw_ready, 1)
            ctx_high(first.after(2))
            for p in range(2):
                act.wait_ge(q_written[p], 96 * NG // 2)

            def turn(b):
                if has(b):
                    exps(b, 0)
                if has(b.after(-1)):
                    out_copy(b.after(-1), 2)
                if has(b.after(2)):
                    key_high(b.after(2))
                if has(b):
                    exps(b, 1)
                if has(b.after(-1)):
                    out_copy(b.after(-1), 3)
                if has(b.after(3)):
                    ctx_high(b.after(3))
                if has(b):
                    exps(b, 2)
                    out_copy(b, 0)
                if has(b.after(1)):
                    value_high(b.after(1))
                if has(b):
                    exps(b, 3)
                    out_copy(b, 1)
                if has(b.after(-1)):
                    attn_high(b.after(-1))

            turn(first)
            turn(first.after(1))
            with act.Fori(0, LOOPS) as i:
                for off in (2, 3):
                    turn(Batch(i, off))
            for b in range(2 + 2 * LOOPS, B + 1):
                turn(Batch(0, b))

            def flat_high(g):
                act.wait_ge(ft_done, g + 1)
                act.copy(group(fh, g), ps[:, BK_T, :].rearrange("p (k n) -> p k n", k=KD)).then_inc(fh_ready, 1)

            def silu(s, par):
                act.wait_ge(h_done, s + 1)
                if not isinstance(s, int) or s >= 2:
                    act.wait_ge(hl_ready, s - 1)
                    act.wait_ge(y_done, s - 1)
                src = ps[:, 2 * par:2 * par + 2, :].rearrange("p a (b n) -> p (a b) n", b=2)
                act.activation(hf[par][:, :, :], src, ACT.Silu).then_inc(hf_ready, 1)
                act.activation(hh[par][:, :, :], src, ACT.Silu).then_inc(hh_ready, 1)

            flat_high(0)
            for g in range(NTG):
                if g + 1 < NTG:
                    flat_high(g + 1)
                silu(g, g % 2)
                act.wait_ge(shifted_ready, g + 1)
                act.activation(gates[2][:, :, :], gates[1][:, :, :], ACT.Exp).then_inc(gate_exp, 1)
            with act.Fori(0, 3) as i:
                for j in range(2 * NTG):
                    silu(2 * NTG * i + NTG + j, (j + 1) % 2)
            for s in range(STEPS - NTG, STEPS):
                silu(s, s % 2)

        @block.vector
        def _(dve):
            def attn_weight_low(n):
                dve.wait_ge(wh_ready, n + 1)
                dve.tensor_tensor(wl[:, n, :, :], wraw[n], wh[:, n, :, :].bitcast(F32), ALU.subtract)\
                    .then_inc(wl_ready, 1)

            def masks(b):
                dve.wait_ge(ctx_in[b.par], 48 * (b.turn + 1))
                if early(b, 2):
                    dve.wait_ge(zeros_set, 1)
                else:
                    dve.wait_ge(stacked[b.par][1], 64 * b.turn)
                dve.tensor_scalar(keep[b.par][:, :], m_raw[b.par][:, :], 0.0, None, ALU.not_equal)\
                    .then_inc(keep_ready, 1)
                dve.wait_ge(keep_ready, b.n + 1)
                dve.tensor_scalar(m_row[b.par][:, :], keep[b.par][0:2, :], mask_c[:, 0:1], mask_c[:, 1:2],
                                  ALU.mult, ALU.add).then_inc(mrow_ready, 1)

            def keys(b):
                for t in range(KD):
                    dve.wait_ge(kproj_done, 2 * b.n + t + 1)
                    if t == 0 and not early(b, 1):
                        dve.wait_ge(kl_ready, b.n)
                    dve.scalar_tensor_tensor(out=kf[:, t, :], in0=ps[:, BK_KV + t, 0:CP], scalar=bk_c[:, t:t + 1],
                                             in1=keep[b.par][:, :], op0=ALU.add, op1=ALU.mult)\
                        .then_inc(kf_ready, 1)

            def values(b):
                if not early(b, 1):
                    dve.wait_ge(vl_ready, b.n)
                dve.wait_ge(vproj_done, 2 * b.n + 1)
                dve.tensor_tensor(vf[:, 0:2, :], ps[0:CT, BK_KV, :].rearrange("p (k n) -> p k n", k=2),
                                  bv_b[0:CT, :].rearrange("p (a n) -> p a n", a=1).to_broadcast([CT, 2, D]),
                                  ALU.add).then_inc(vf_ready, 1)
                dve.wait_ge(vproj_done, 2 * b.n + 2)
                dve.tensor_tensor(vf[:, 2, :], ps[0:CT, BK_KV + 1, 0:D], bv_b[0:CT, :], ALU.add)\
                    .then_inc(vf_ready, 1)

            def attn_low(b):
                dve.wait_ge(th_ready, b.n + 1)
                col = bass.ds(S * b.n, S)
                dve.tensor_tensor(tl[:, :, col], ps[:, BK_AT, 0:KD * S].rearrange("p (k n) -> p k n", k=KD),
                                  th[:, :, col].bitcast(F32), ALU.subtract).then_inc(tl_ready, 1)

            def max_rows(b):
                dve.wait_ge(maxt_done, b.n + 1)
                if not early(b, 1):
                    before = b.after(-1)
                    dve.wait_ge(mx_stacked[before.par], 32 * (before.turn + 1))
                dve.tensor_copy(mx_h[:, :], ps[0:H, BK_MAX, 0:S]).then_inc(mx_ready, 1)
                dve.wait_ge(mx_ready, 2 * b.n + 1)
                dve.tensor_tensor(mx_l[:, :], ps[0:H, BK_MAX, 0:S], mx_h[:, :].bitcast(F32), ALU.subtract)\
                    .then_inc(mx_ready, 1)

            def maxima(b, heads):
                for h in heads:
                    dve.wait_ge(smax_done, H * b.n + h + 1)
                    if h == 0 and not early(b, 1):
                        dve.wait_ge(maxt_done, b.n)
                    dve.tensor_reduce(neg_max[:, h:h + 1], ps[0:S, BK_MAX + h % 2, 0:CP], AX.X, ALU.max,
                                      negate=True).then_inc(max_read, 1)

            def probs_low(b, j):
                dve.wait_ge(ph_ready, QUADS * b.n + j + 1)
                dve.tensor_tensor(pl[j % 2][:, :, :], pf[j % 2][:, :, :], ph[j % 2][:, :, :].bitcast(F32),
                                  ALU.subtract).then_inc(pl_even, 1)

            def normalise(b):
                dve.wait_ge(ott_done, b.n + 1)
                o = ps[0:S, BK_KV:BK_KV + 2, 0:8 * OW].rearrange("p k (h d) -> p k h d", h=8)
                r = rsum[:, :].rearrange("p (k h) -> p k h", k=2)
                dve.reciprocal(r, o[:, :, :, 2 * DK]).then_inc(rsum_ready, 1)
                dve.wait_ge(rsum_ready, b.n + 1)
                if not early(b, 1):
                    dve.wait_ge(at_done, b.n)
                wide = rsum[:, :].rearrange("p (k h a) -> p k h a", k=2, a=1).to_broadcast([S, 2, 8, DK])
                for part, dst in ((0, ah), (1, al)):
                    dve.tensor_tensor(dst[:, :].rearrange("p (h k d) -> p k h d", k=2, h=8),
                                      o[:, :, :, DK * part:DK * (part + 1)], wide, ALU.mult).then_inc(o_read, 1)

            first = Batch(0, 0)
            dve.memset(mask_c[:, 0:1], -NEG_LO)
            dve.memset(mask_c[:, 1:2], NEG_LO).then_inc(const_set, 1)
            dve.wait_ge(const_set, 1)
            dve.memset(mask_c[0:1, 0:1], -NEG_HI)
            for e in range(E):
                dve.memset(pos[:, :, e:e + 1], float(E - e))
            dve.memset(mask_c[0:1, 1:2], NEG_HI).then_inc(const_set, 1)
            dve.wait_ge(const_set, 2)
            attn_weight_low(0)
            masks(first)
            attn_weight_low(1)
            dve.wait_ge(bias_in, 64)
            dve.wait_ge(xr_in, 16)
            for b in range(B):
                dve.bn_stats(stats[0:S, b, :], xr[:, b, :]).then_inc(stats_ready, 1)
            for b in range(B):
                dve.wait_ge(stats_ready, b + 1)
                dve.bn_aggr(moments[0:S, b, :], stats[0:S, b, :]).then_inc(mom_ready, 1)
            keys(first)
            values(first)
            masks(first.after(1))
            attn_weight_low(2)
            dve.wait_ge(std_ready, 1)
            dve.reciprocal(rstd[0:S, :], std[0:S, :]).then_inc(rstd_ready, 1)
            dve.wait_ge(rstd_ready, 1)

            def normalise_x(g):
                for b in range(GB * g, GB * (g + 1)):
                    dve.tensor_scalar(xr[:, b, :], xr[:, b, :], moments[0:S, b, 0:1], rstd[0:S, b:b + 1],
                                      ALU.subtract, ALU.mult).then_inc(xn_ready, 1)

            def x_low(g):
                dve.wait_ge(xh_ready, g + 1)
                dve.tensor_tensor(xl[g % 2][:, :, :], ps[:, 0:2, 0:SG], xh[g % 2][:, :, :].bitcast(F32),
                                  ALU.subtract).then_inc(xl_ready, 1)

            def queries(g):
                for t in range(KD):
                    dve.wait_ge(qproj_done, 2 * g + t + 1)
                    if g and t == 0:
                        dve.wait_ge(ql_ready, g)
                    dve.tensor_scalar(qf[:, t, :], ps[:, (2, BK_OUT)[t], 0:SG], bq_c[:, t:t + 1], DK ** -0.5,
                                      ALU.add, ALU.mult).then_inc(qf_ready, 1)
                dve.wait_ge(qh_ready, g + 1)
                dve.tensor_tensor(ql[g % 2][:, :, :], qf[:, :, :], qh[g % 2][:, :, :].bitcast(F32), ALU.subtract)\
                    .then_inc(ql_ready, 1)

            normalise_x(0)
            x_low(0)
            keys(first.after(1))
            normalise_x(1)
            for g in range(NG):
                if g + 1 < NG:
                    x_low(g + 1)
                if g + 2 < NG:
                    normalise_x(g + 2)
                queries(g)
            attn_weight_low(3)
            dve.wait_ge(rw_ready, 1)
            dve.tensor_tensor(rwl[:, :, :], rw_raw[:, :, :], rwh[:, :, :].bitcast(F32), ALU.subtract)\
                .then_inc(rw_ready, 1)
            masks(first.after(2))
            keys(first.after(2))
            maxima(first, range(H))
            max_rows(first)

            def turn(b):
                after, before = b.after(1), b.after(-1)
                if has(after):
                    maxima(after, range(0, 4))
                    values(after)
                    maxima(after, range(4, 10))
                if has(b):
                    probs_low(b, 0)
                if has(after):
                    maxima(after, range(10, 12))
                if has(b.after(3)):
                    masks(b.after(3))
                if has(before):
                    normalise(before)
                if has(after):
                    maxima(after, range(12, H))
                    max_rows(after)
                if has(b):
                    probs_low(b, 2)
                if has(b.after(3)):
                    keys(b.after(3))
                if has(before):
                    attn_low(before)

            turn(first)
            turn(first.after(1))
            with dve.Fori(0, LOOPS) as i:
                for off in (2, 3):
                    turn(Batch(i, off))
            for b in range(2 + 2 * LOOPS, B + 1):
                turn(Batch(0, b))

            n_steps = [0]

            def step(ins):
                n_steps[0] += 1
                ins.then_inc(chain_step, 1)
                dve.wait_ge(chain_step, n_steps[0])

            def layernorm(g):
                dve.wait_ge(oproj_done, g + 1)
                dve.wait_ge(xb_ready, g + 1)
                dve.tensor_tensor(x2[:, 2 * g:2 * g + 2, :], ps[:, BK_A, :].rearrange("p (n d) -> p n d", n=2),
                                  x2[:, 2 * g:2 * g + 2, :], ALU.add).then_inc(resid_added, 1)
                dve.wait_ge(resid_added, g + 1)
                dve.bn_stats(st2[:, 0, :], x2[:, 2 * g, :])
                step(dve.bn_stats(st2[:, 1, :], x2[:, 2 * g + 1, :]))
                dve.bn_aggr(mo2[:, 0, :], st2[:, 0, :])
                step(dve.bn_aggr(mo2[:, 1, :], st2[:, 1, :]))
                var, r, t, u = nw
                step(dve.tensor_scalar(var[:, :], mo2[:, :, 1], LN_EPS, None, ALU.add))
                step(dve.tensor_scalar(t[:, :].bitcast(I32), var[:, :].bitcast(I32), 1, None,
                                       ALU.logical_shift_right))
                step(dve.tensor_scalar(r[:, :].bitcast(I32), t[:, :].bitcast(I32), -1.0, float(MAGIC),
                                       ALU.mult, ALU.add))
                for _ in range(4):
                    step(dve.tensor_tensor(t[:, :], r[:, :], r[:, :], ALU.mult))
                    step(dve.scalar_tensor_tensor(out=u[:, :], in0=t[:, :], scalar=-0.5, in1=var[:, :],
                                                  op0=ALU.mult, op1=ALU.mult))
                    step(dve.scalar_tensor_tensor(out=r[:, :], in0=u[:, :], scalar=1.5, in1=r[:, :],
                                                  op0=ALU.add, op1=ALU.mult))
                if g >= 2:
                    dve.wait_ge(ft_done, g - 1)
                for a in range(2):
                    last = dve.tensor_scalar(xn2[g % 2][:, a, :], x2[:, 2 * g + a, :], mo2[:, a, 0:1], r[:, a:a + 1],
                                             ALU.subtract, ALU.mult)
                last.then_inc(xn2_ready, 1)
                dve.wait_ge(xn2_ready, g + 1)

            def flat_low(g):
                dve.wait_ge(fh_ready, g + 1)
                dve.tensor_tensor(group(fl, g), ps[:, BK_T, :].rearrange("p (k n) -> p k n", k=KD),
                                  group(fh, g).bitcast(F32), ALU.subtract).then_inc(fl_ready, 1)

            logits, shifted, expd, picked, rest, t0, t1 = gates
            c0, c1, c2, c3 = gcol

            def wide2(col):
                return col[:, :].rearrange("p (n a) -> p n a", a=1).to_broadcast([P, 2, E])

            def first_of(src, col, dst):
                step(dve.tensor_tensor(t0[:, :, :], src, wide2(col), ALU.is_equal))
                step(dve.tensor_tensor(t1[:, :, :], t0[:, :, :], pos[:, :, :], ALU.mult))
                step(dve.tensor_reduce(c1[:, :], t1[:, :, :], AX.X, ALU.max))
                step(dve.tensor_tensor(dst, t1[:, :, :], wide2(c1), ALU.is_equal))

            def pick(g):
                dve.wait_ge(route_done, g + 1)
                dve.tensor_copy(logits[:, :, :], ps[:, BK_T, 0:2 * E].rearrange("p (n e) -> p n e", n=2))\
                    .then_inc(logits_read, 1)
                dve.wait_ge(logits_read, g + 1)
                step(dve.tensor_reduce(c0[:, :], logits[:, :, :], AX.X, ALU.max))
                dve.tensor_tensor(shifted[:, :, :], logits[:, :, :], wide2(c0), ALU.subtract)\
                    .then_inc(shifted_ready, 1)
                first_of(logits[:, :, :], c0, picked[:, :, :])
                step(dve.scalar_tensor_tensor(out=rest[:, :, :], in0=picked[:, :, :], scalar=-3.0e38,
                                              in1=logits[:, :, :], op0=ALU.mult, op1=ALU.add))
                step(dve.tensor_reduce(c2[:, :], rest[:, :, :], AX.X, ALU.max))
                second = cw[:, 2 * g:2 * g + 2, :]
                first_of(rest[:, :, :], c2, second)
                step(dve.tensor_tensor(picked[:, :, :], picked[:, :, :], second, ALU.add))

            def weigh(g):
                dve.wait_ge(gate_exp, g + 1)
                step(dve.tensor_reduce(c0[:, :], expd[:, :, :], AX.X, ALU.add))
                step(dve.reciprocal(c1[:, :], c0[:, :]))
                step(dve.tensor_tensor(t0[:, :, :], expd[:, :, :], wide2(c1), ALU.mult))
                step(dve.tensor_tensor(t1[:, :, :], t0[:, :, :], picked[:, :, :], ALU.mult))
                step(dve.tensor_reduce(c2[:, :], t1[:, :, :], AX.X, ALU.add))
                step(dve.tensor_scalar(c3[:, :], c2[:, :], GATE_EPS, None, ALU.max))
                step(dve.reciprocal(c0[:, :], c3[:, :]))
                step(dve.tensor_tensor(cw[:, 2 * g:2 * g + 2, :], t1[:, :, :], wide2(c0), ALU.mult))

            def h_low(s, par):
                dve.wait_ge(hh_ready, s + 1)
                dve.tensor_tensor(hl[par][:, :, :], hf[par][:, :, :], hh[par][:, :, :].bitcast(F32),
                                  ALU.subtract).then_inc(hl_ready, 1)

            def add_y(s, e, g, par):
                dve.wait_ge(y_done, s + 1)
                if not isinstance(s, int) or s >= NTG:
                    dve.wait_ge(y_added, 2 * (s - NTG + 1))
                for a in range(2):
                    n = 2 * g + a
                    dve.scalar_tensor_tensor(out=x2[:, n, :], in0=ps[:, BK_Y + par, D * a:D * a + D],
                                             scalar=cw[:, n, bass.ds(e, 1)], in1=x2[:, n, :],
                                             op0=ALU.mult, op1=ALU.add).then_inc(y_added, 1)

            layernorm(0)
            layernorm(1)
            flat_low(0)
            for g in range(NTG):
                pick(g)
                if g + 1 < NTG:
                    flat_low(g + 1)
                h_low(g, g % 2)
                if g + 2 < NTG:
                    layernorm(g + 2)
                if g >= 1:
                    add_y(g - 1, 0, g - 1, (g - 1) % 2)
                weigh(g)
            with dve.Fori(0, 3) as i:
                for j in range(2 * NTG):
                    s = 2 * NTG * i + NTG + j
                    h_low(s, (j + 1) % 2)
                    add_y(s - 1, 2 * i + (j + NTG - 1) // NTG, (j - 1) % NTG, j % 2)
            for s in range(STEPS - NTG, STEPS):
                h_low(s, s % 2)
                add_y(s - 1, (s - 1) // NTG, (s - 1) % NTG, (s - 1) % 2)
            add_y(STEPS - 1, E - 1, NTG - 1, (STEPS - 1) % 2)

        @block.tensor
        def _(pe):
            def product(o, terms):
                for n, (lhs, rhs) in enumerate(terms):
                    last = pe.matmul(o, lhs, rhs, start=n == 0, stop=n == len(terms) - 1)
                return last

            def project_keys(b):
                pe.wait_ge(ch_ready, b.n + 1)
                pe.wait_ge(cl_ready, b.n + 1)
                if early(b, 4):
                    if b.n:
                        pe.wait_ge(*{1: (vf_ready, 2), 2: (kf_ready, 4), 3: (vf_ready, 4)}[b.n])
                else:
                    pe.wait_ge(o_read, 2 * (b.n - 3))
                for t in range(KD):
                    m = slice(t * P, (t + 1) * P)
                    product(ps[:, BK_KV + t, 0:CP],
                            [(w[:, 0, k, m], c[b.par][:, k, :]) for k in range(KD)
                             for w, c in ((wh, ch), (wl, ch), (wh, cl))]).then_inc(kproj_done, 1)

            def project_values(b, k3):
                if k3 == 0:
                    if early(b, 1):
                        pe.wait_ge(kf_ready, 2)
                    elif has(b.after(1)):
                        pe.wait_ge(kf_ready, 2 * (b.n + 2))
                    else:
                        pe.wait_ge(o_read, 2 * (b.n - 2))
                m = slice(k3 * CT, (k3 + 1) * CT)
                last = product(ps[0:CT, BK_KV + k3 // 2, D * (k3 % 2):D * (k3 % 2) + D],
                               [(c[b.par][:, k, m], w[:, 1, k, :]) for k in range(KD)
                                for w, c in ((wh, ch), (wh, cl), (wl, ch))])
                if k3 != 0:
                    last.then_inc(vproj_done, 1)

            def head_scores(b, heads):
                for h in heads:
                    if h % HALF == 0:
                        pe.wait_ge(stacked[b.par][h // HALF], 64 * (b.turn + 1))
                    if h >= 2:
                        pe.wait_ge(max_read, H * b.n + h - 1)
                    elif h == 0 and not early(b, 1):
                        pe.wait_ge(mx_ready, 2 * b.n)
                    elif h == 1 and not early(b, 3):
                        pe.wait_ge(tl_ready, b.n - 2)
                    pe.matmul(ps[0:S, BK_MAX + h % 2, 0:CP],
                              qs[b.par][0:R_MAX, h // 2, S * (h % 2):S * (h % 2) + S],
                              ks[b.par][0:R_MAX, h // 2, :], start=True, stop=True).then_inc(smax_done, 1)

            def max_transpose(b):
                pe.wait_ge(max_read, H * (b.n + 1))
                pe.transpose(ps[0:H, BK_MAX, 0:S], neg_max[:, :], ident[0:S, 0:S]).then_inc(maxt_done, 1)

            def quad_scores(b, j):
                if j == 0:
                    pe.wait_ge(mx_stacked[b.par], 32 * (b.turn + 1))
                if not (early(b, 1) and j < 1):
                    pe.wait_ge(ph_ready, QUADS * b.n + j)
                for k3 in range(KT):
                    for q in range(2):
                        last = pe.matmul(ps[0:CT, BK_ST + k3, 2 * S * q:2 * S * (q + 1)],
                                         ks[b.par][0:ROWS, 2 * j + q, k3 * CT:(k3 + 1) * CT],
                                         qs[b.par][0:ROWS, 2 * j + q, :], start=True, stop=True)
                last.then_inc(st_done, 1)

            def quad_outputs(b, j):
                pe.wait_ge((pl_even, pl_odd)[j % 2], 2 * b.n + j // 2 + 1)
                if j == 0:
                    pe.wait_ge(vl_ready, b.n + 1)
                if not (early(b, 1) and j < 1):
                    pe.wait_ge(ot_ready, QUADS * b.n + j)
                for q in range(2):
                    cols = slice(2 * S * q, 2 * S * (q + 1))
                    last = product(ps[0:VM, BK_OUT, cols],
                                   [(vs[b.par][:, k3, 2 * j + q, 0:VM], part[j % 2][:, k3, cols])
                                    for k3 in range(KT) for part in (ph, pl)])
                last.then_inc(pv_done, 1)

            def out_transpose(b):
                pe.wait_ge(ot_ready, QUADS * (b.n + 1))
                if has(b.after(2)):
                    pe.wait_ge(vf_ready, 2 * (b.n + 3))
                else:
                    pe.wait_ge(o_read, 2 * b.n)
                for h in range(H):
                    rows = slice(A1 * (h % 2), A1 * (h % 2) + OW) if h else slice(0, VM)
                    c = OW * (h // 2)
                    last = pe.transpose(ps[0:S, BK_KV + h % 2, c:c + rows.stop - rows.start],
                                        ot[h // 4][rows, S * (h % 4):S * (h % 4 + 1)], ident[rows, rows])
                last.then_inc(ott_done, 1)

            def attn_transpose(b):
                pe.wait_ge(an_ready, b.n + 1)
                if not has(b.after(2)):
                    pe.wait_ge(tl_ready, b.n)
                for k in range(KD):
                    last = pe.transpose(ps[:, BK_AT, S * k:S * (k + 1)], ah[:, k * P:(k + 1) * P], ident[0:S, 0:S])
                last.then_inc(at_done, 1)

            def turn(b):
                after, before = b.after(1), b.after(-1)
                if has(b):
                    quad_scores(b, 0)
                if has(before):
                    quad_outputs(before, 2)
                if has(after):
                    head_scores(after, range(0, 2))
                    project_values(after, 0)
                    head_scores(after, range(2, 3))
                    project_values(after, 1)
                    head_scores(after, range(3, 4))
                    project_values(after, 2)
                    head_scores(after, range(4, 5))
                if has(b):
                    quad_scores(b, 1)
                if has(before):
                    quad_outputs(before, 3)
                if has(after):
                    head_scores(after, range(5, 10))
                if has(b):
                    quad_scores(b, 2)
                if has(after):
                    head_scores(after, range(10, 12))
                if has(b):
                    quad_outputs(b, 0)
                if has(before):
                    out_transpose(before)
                if has(after):
                    head_scores(after, range(12, H))
                if has(b):
                    quad_scores(b, 3)
                if has(after):
                    max_transpose(after)
                if has(b):
                    quad_outputs(b, 1)
                if has(b.after(3)):
                    project_keys(b.after(3))
                if has(before):
                    attn_transpose(before)

            first = Batch(0, 0)
            pe.wait_ge(wl_ready, 1)
            project_keys(first)
            pe.wait_ge(wl_ready, 2)
            for k3 in range(KT):
                project_values(first, k3)
            project_keys(first.after(1))

            def x_transpose(g):
                pe.wait_ge(xn_ready, GB * (g + 1))
                if g == 0:
                    pe.wait_ge(ident_set, 2)
                else:
                    pe.wait_ge(xl_ready, g)
                for k in range(KD):
                    for b in range(GB):
                        last = pe.transpose(ps[:, k, S * b:S * (b + 1)], xr[:, GB * g + b, k * P:(k + 1) * P],
                                            ident[0:S, 0:S])
                last.then_inc(xt_done, 1)

            def project_queries(g):
                pe.wait_ge(wl_ready, 3)
                pe.wait_ge(xl_ready, g + 1)
                for t in range(KD):
                    if g >= 1:
                        pe.wait_ge(qf_ready, 2 * g - 1 + t)
                    m = slice(t * P, (t + 1) * P)
                    product(ps[:, (2, BK_OUT)[t], 0:SG],
                            [(w[:, 2, k, m], x[g % 2][:, k, :]) for k in range(KD)
                             for w, x in ((wh, xh), (wl, xh), (wh, xl))]).then_inc(qproj_done, 1)

            x_transpose(0)
            for g in range(NG):
                if g + 1 < NG:
                    x_transpose(g + 1)
                project_queries(g)
            project_keys(first.after(2))
            pe.wait_ge(filled, N_FILLS)
            head_scores(first, range(H))
            max_transpose(first)
            turn(first)
            turn(first.after(1))
            with pe.Fori(0, LOOPS) as i:
                for off in (2, 3):
                    turn(Batch(i, off))
            for b in range(2 + 2 * LOOPS, B + 1):
                turn(Batch(0, b))

            def project_output(g):
                if g >= 1:
                    pe.wait_ge(resid_added, g)
                for a in range(2):
                    m = slice((2 * g + a) * P, (2 * g + a + 1) * P)
                    last = product(ps[:, BK_A, D * a:D * (a + 1)],
                                   [(x[:, k, m], w[:, 3, k, :]) for k in range(KD)
                                    for x, w in ((th, wh), (th, wl), (tl, wh))])
                last.then_inc(oproj_done, 1)

            def flat_transpose(g):
                pe.wait_ge(xn2_ready, g + 1)
                if g >= 1:
                    pe.wait_ge(logits_read, g)
                for k in range(KD):
                    for a in range(2):
                        last = pe.transpose(ps[:, BK_T, TG * k + P * a:TG * k + P * (a + 1)],
                                            xn2[g % 2][:, a, k * P:(k + 1) * P], ident[:, :])
                last.then_inc(ft_done, 1)

            def route(g):
                pe.wait_ge(fl_ready, g + 1)
                for a in range(2):
                    m = slice((2 * g + a) * P, (2 * g + a + 1) * P)
                    last = product(ps[:, BK_T, E * a:E * (a + 1)],
                                   [(f[:, k, m], w[:, k, :]) for k in range(KD)
                                    for f, w in ((fh, rwh), (fh, rwl), (fl, rwh))])
                last.then_inc(route_done, 1)

            def hidden(s, g, par, wpar, e):
                if g == 0:
                    pe.wait_ge(ew_ready, 4 * (e + 1))
                if not isinstance(s, int) or s >= 2:
                    pe.wait_ge(hh_ready, s - 1)
                m = slice(g * TG, (g + 1) * TG)
                for f in range(KF):
                    c = slice(f * P, (f + 1) * P)
                    last = product(ps[:, 2 * par + f // 2, TG * (f % 2):TG * (f % 2 + 1)],
                                   [(w[wpar][:, k, c], x[:, k, m]) for k in range(KD)
                                    for w, x in ((w1h, fh), (w1l, fh), (w1h, fl))])
                last.then_inc(h_done, 1)

            def expert_out(s, par, wpar):
                pe.wait_ge(hl_ready, s + 1)
                if not isinstance(s, int) or s >= 2:
                    pe.wait_ge(y_added, 2 * (s - 1))
                for a in range(2):
                    m = slice(a * P, (a + 1) * P)
                    last = product(ps[:, BK_Y + par, D * a:D * (a + 1)],
                                   [(x[par][:, f, m], w[wpar][:, f, :]) for f in range(KF)
                                    for x, w in ((hh, w2h), (hh, w2l), (hl, w2h))])
                last.then_inc(y_done, 1)

            pe.wait_ge(wl_ready, 4)
            pe.wait_ge(th_ready, B)
            pe.wait_ge(tl_ready, B)
            project_output(0)
            project_output(1)
            flat_transpose(0)
            pe.wait_ge(rw_ready, 2)
            for g in range(NTG):
                route(g)
                if g + 2 < NTG:
                    project_output(g + 2)
                if g + 1 < NTG:
                    flat_transpose(g + 1)
                hidden(g, g, g % 2, 0, 0)
                if g >= 1:
                    expert_out(g - 1, (g - 1) % 2, 0)
            with pe.Fori(0, 3) as i:
                for j in range(2 * NTG):
                    s = 2 * NTG * i + NTG + j
                    hidden(s, j % NTG, (j + 1) % 2, (1 + j // NTG) % 2, 2 * i + 1 + j // NTG)
                    expert_out(s - 1, j % 2, ((j + NTG - 1) // NTG) % 2)
            for s in range(STEPS - NTG, STEPS):
                hidden(s, s % NTG, s % 2, (E - 1) % 2, E - 1)
                expert_out(s - 1, (s - 1) % 2, ((s - 1) // NTG) % 2)
            expert_out(STEPS - 1, (STEPS - 1) % 2, (E - 1) % 2)


def kernel(x, ctx_1024, mask_BxS2_ik0, L0_xattn_Wq, L0_xattn_bq, L0_xattn_Wk, L0_xattn_bk, L0_xattn_Wv,
           L0_xattn_bv, L0_xattn_Wo, L0_xattn_bo, L0_ffn_router_w, L0_ffn_w1, L0_ffn_w2):
    import numpy as np
    import concourse.bacc as bacc
    from concourse.bass_utils import run_bass_kernel_spmd

    def halves(w):
        return np.ascontiguousarray(np.asarray(w)).reshape(KD, P, -1)

    x = np.asarray(x)
    arrays = {
        "x_rows": x,
        "x_tiles": x.reshape(NT, P, D),
        "ctx_t": np.ascontiguousarray(np.asarray(ctx_1024).transpose(2, 0, 1)).reshape(KD, P, B, C),
        "mask": np.asarray(mask_BxS2_ik0),
        "wq_t": halves(np.asarray(L0_xattn_Wq).T),
        "wk_t": halves(np.asarray(L0_xattn_Wk).T),
        "wv_t": halves(np.asarray(L0_xattn_Wv).T),
        "wo_t": halves(np.asarray(L0_xattn_Wo).T),
        "bq": np.ascontiguousarray(np.asarray(L0_xattn_bq).reshape(KD, P).T),
        "bk": np.ascontiguousarray(np.asarray(L0_xattn_bk).reshape(KD, P).T),
        "bv": np.asarray(L0_xattn_bv).reshape(1, D),
        "bo": np.asarray(L0_xattn_bo).reshape(1, D),
        "router_w": halves(L0_ffn_router_w),
        "w1": np.ascontiguousarray(np.asarray(L0_ffn_w1)).reshape(E, KD, P, F),
        "w2": np.ascontiguousarray(np.asarray(L0_ffn_w2)).reshape(E, KF, P, D),
    }
    nc = bacc.Bacc("TRN2", target_bir_lowering=False, num_devices=1)
    args = [nc.dram_tensor(n, a.shape, mybir.dt.from_np(a.dtype), kind="ExternalInput").ap()
            for n, a in arrays.items()]
    args.append(nc.dram_tensor("out", (NT, P, D), F32, kind="ExternalOutput").ap())
    xattn_moe_kernel(nc, *args)
    r = run_bass_kernel_spmd(nc, [arrays], core_ids=[0])
    return np.asarray(r.results[0]["out"]).reshape(B, S, D)
```

```python
from contextlib import ExitStack

import concourse.bass as bass
from concourse import mybir

F32 = mybir.dt.float32
F32R = mybir.dt.float32r
I32 = mybir.dt.int32
ALU = mybir.AluOpType
ACT = mybir.ActivationFunctionType
AX = mybir.AxisListType

P = 128
B, S, D = 16, 112, 256
C = 375
CP = C + 1
H, DK = 16, 16
E, F = 8, 512
KD = D // P
KF = F // P
KT = 3
CT = C // KT
PAIRS = H // 2
QUADS = H // 4
T = B * S
NT = T // P
GB = 4
NG = B // GB
SG = GB * S
TG = 2 * P
NTG = T // TG
TOP = 2
STEPS = T * TOP // TG + E - 1
LOOP_STEPS = (STEPS - 5) // 2
NEG = -1.0e9
NEG_HI = -1000079360.0
NEG_LO = NEG - NEG_HI
LN_EPS = 1e-5
GATE_EPS = 1e-9

PARTS = 3
HALF = H // 2
R_MASK, R_MAX, ROWS = 96, 98, 100

A1 = 64
VM = A1 + 2 * DK + 1
VW = VM + 1
OW = 2 * DK + 1
MAGIC = 0x5f3759df

BK_ST, BK_MAX, BK_KV, BK_OUT = 0, 3, 5, 7
BK_AT = BK_MAX + 1
BK_T, BK_LT, BK_L, BK_RANK, BK_Y = 6, 5, 4, 6, 4
N_FILLS = 10
LOOPS = (B - 6) // 2


class Batch:

    def __init__(self, i, off):
        self.i, self.off = i, off
        self.par, self.turn, self.n = off % 2, i + off // 2, 2 * i + off

    def after(self, k):
        return Batch(self.i, self.off + k)


def xattn_moe_kernel(nc, x_rows, x_tiles, ctx_t, mask, wq_t, wk_t, wv_t, wo_t, bq, bk, bv, bo,
                     router_w, w1, w2, out):
    ctx = ExitStack()
    with ctx:
        def sem(name):
            return ctx.enter_context(nc.semaphore(name))

        base = (nc.sbuf_base + 63) // 64 * 64
        cursor = {"at": base, "top": base}

        def sb(name, shape, dt=F32):
            size = 4
            for n in shape[1:]:
                size *= n
            off = cursor["at"]
            cursor["at"] += (size + 63) // 64 * 64
            cursor["top"] = max(cursor["top"], cursor["at"])
            return nc.alloc_sbuf_tensor_at(name, shape, dt, offset=off)

        ident = sb("ident", [P, P])
        th = sb("attn_t_hi", [P, KD, T], F32R)
        tl = sb("attn_t_lo", [P, KD, T], F32R)
        wh = sb("attn_w_hi", [P, 4, KD, D], F32R)
        wl = sb("attn_w_lo", [P, 4, KD, D], F32R)
        rw_raw = sb("router_raw", [P, KD, E])
        rwh = sb("router_hi", [P, KD, E], F32R)
        rwl = sb("router_lo", [P, KD, E], F32R)
        bv_b = sb("bv_b", [P, D])
        bo_b = sb("bo_b", [P, D])
        bq_c = sb("bq_c", [P, KD])
        bk_c = sb("bk_c", [P, KD])
        mask_c = sb("mask_c", [2, 2])
        stats = sb("stats", [P, B, 6])
        moments = sb("moments", [P, B, 2])
        std = sb("std", [P, B])
        rstd = sb("rstd", [P, B])
        pos = sb("gate_pos", [P, NT, E])
        eps_c = sb("eps_c", [P, 1])
        w_raw0 = sb("w1_raw0", [P, KD, F]), sb("w2_raw0", [P, KF, D])
        wraw = [w_raw0[0][:, 0:2, 0:256], w_raw0[0][:, 0:2, 256:512],
                w_raw0[1][:, 0:2, :], w_raw0[1][:, 2:4, :]]

        shared = cursor["at"]
        xh = [sb(f"x_t_hi{p}", [P, KD, SG], F32R) for p in range(2)]
        xl = [sb(f"x_t_lo{p}", [P, KD, SG], F32R) for p in range(2)]
        q_end = cursor["at"]

        def expert_buffers(p):
            return (sb(f"w1_hi{p}", [P, KD, F], F32R), sb(f"w1_lo{p}", [P, KD, F], F32R),
                    sb(f"w2_hi{p}", [P, KF, D], F32R), sb(f"w2_lo{p}", [P, KF, D], F32R))

        cursor["at"] = shared
        expert_even = expert_buffers(0)
        cursor["at"] = max(q_end, cursor["at"])

        attn_start = cursor["at"]
        c_raw = [sb(f"ctx_raw{p}", [P, KD, CP]) for p in range(2)]
        ch = [sb(f"ctx_hi{p}", [P, KD, CP], F32R) for p in range(2)]
        cl = [sb(f"ctx_lo{p}", [P, KD, CP], F32R) for p in range(2)]
        m_raw = [sb(f"mask_raw{p}", [P, CP], I32) for p in range(2)]
        keep = [sb(f"keep{p}", [P, CP]) for p in range(2)]
        m_row = [sb(f"mask_row{p}", [2, CP], F32R) for p in range(2)]
        kf = sb("k_f32", [P, KD, CP])
        kh = sb("k_hi", [P, KD, CP], F32R)
        kl = sb("k_lo", [P, KD, CP], F32R)
        ks = [sb(f"k_stack{p}", [P, PAIRS, CP], F32R) for p in range(2)]
        qs = [sb(f"q_stack{p}", [P, PAIRS, 2 * S], F32R) for p in range(2)]
        vf = sb("v_f32", [CT, KT, D])
        vs = [sb(f"v_stack{p}", [CT, KT, PAIRS, VW], F32R) for p in range(2)]
        probs_at = cursor["at"]
        pf, ph, pl = [None] * 2, [None] * 2, [None] * 2
        for p in range(2):
            pf[p] = sb(f"probs_f32{p}", [CT, KT, 4 * S])
            ph[p] = sb(f"probs_hi{p}", [CT, KT, 4 * S], F32R)
        for p in range(2):
            pl[p] = sb(f"probs_lo{p}", [CT, KT, 4 * S], F32R)
        ot_at = cursor["at"]
        ot = [sb(f"out_t{n}", [VM, 4 * S]) for n in range(QUADS)]
        neg_max = sb("neg_max", [S, H])
        mx_h = sb("max_hi", [H, S], F32R)
        mx_l = sb("max_lo", [H, S], F32R)
        rsum = sb("rsum", [S, H])
        ah = sb("attn_rows", [S, D])
        al = sb("attn_rows_by_lo", [S, D])
        attn_end = cursor["at"]
        cursor["at"] = probs_at
        xr = sb("x_rows_sb", [S, B, D])
        qh = [sb(f"q_hi{p}", [P, KD, SG], F32R) for p in range(2)]
        ql = [sb(f"q_lo{p}", [P, KD, SG], F32R) for p in range(2)]
        assert cursor["at"] <= ot_at
        cursor["at"] = ot_at
        qf = sb("q_f32", [P, KD, SG])
        assert cursor["at"] <= ot_at + 2 * 4 * S * 4
        cursor["at"] = attn_start
        x2 = sb("x2", [P, NT, D])
        assert cursor["at"] <= attn_start + 6 * KD * CP * 4, "x2 lies where the context's parts were"
        hf = [sb(f"h_f32{p}", [P, KF, TG]) for p in range(2)]
        hh = [sb(f"h_hi{p}", [P, KF, TG], F32R) for p in range(2)]
        hl = [sb(f"h_lo{p}", [P, KF, TG], F32R) for p in range(2)]
        fh = [sb(f"flat_t_hi{p}", [P, KD, TG], F32R) for p in range(2)]
        fl = [sb(f"flat_t_lo{p}", [P, KD, TG], F32R) for p in range(2)]
        rows = [sb(f"rows{p}", [P, 2, D]) for p in range(2)]
        yo = [sb(f"y_out{p}", [P, 2, D]) for p in range(2)]
        xn2 = sb("xn2", [P, NT, D])
        chosen = [sb(f"chosen_rows{n}", [P, NT, D]) for n in range(TOP)]
        gates = [sb(f"gate{n}", [P, NT, E]) for n in range(9)]
        both = sb("both_experts", [P, NT + 1, E], F32R)
        gcol = [sb(f"gate_col{n}", [P, NT]) for n in range(4)]
        weight = [sb(f"weight{n}", [P, NT]) for n in range(TOP)]
        place = [sb(f"place{n}", [P, NT], I32) for n in range(TOP)]
        nw = [sb(f"newton{n}", [P, NT]) for n in range(4)]
        st2 = sb("stats2", [P, NT, 6])
        mo2 = sb("moments2", [P, NT, 2])
        rph = sb("router_padded_hi", [P, KD, P], F32R)
        rpl = sb("router_padded_lo", [P, KD, P], F32R)
        logits_t = [sb(f"logits_t{p}", [E, TG]) for p in range(2)]
        zeros = sb("zeros", [P, D])
        ones = sb("ones", [P, P], F32R)
        earlier = sb("earlier", [P, P], F32R)
        block_start = sb("block_start", [P, E, T // TG])
        up_to = sb("up_to", [P, E, E])
        step_no = sb("step_no", [1, STEPS, E])
        counts = sb("counts", [P, E])
        is_block = sb("is_block", [P, E, T // TG])
        blocks = sb("blocks", [P, E])
        blocks_to = sb("blocks_to", [P, E, E])
        block_end = sb("block_end", [P, E])
        blocks_before = sb("blocks_before", [P, E])
        first_row = sb("first_row", [P, E])
        passed = sb("passed", [1, STEPS, E])
        step_expert = sb("step_expert", [1, STEPS])
        expert_of = sb("expert_of_step", [1, STEPS], I32)
        w_raw = w_raw0, (sb("w1_raw1", [P, KD, F]), sb("w2_raw1", [P, KF, D]))
        w1h, w1l, w2h, w2l = zip(expert_even, expert_buffers(1))
        assert cursor["top"] <= nc.sbuf_usable_end, (cursor, nc.sbuf_usable_end)

        ps = ctx.enter_context(nc.psum_tensor("ps", [P, 8, 512], F32))

        k_scratch = [nc.dram_tensor(f"k_scratch{p}", [KD, H // KD, PARTS, DK, CP], F32).ap() for p in range(2)]
        q_scratch = nc.dram_tensor("q_scratch", [KD, H // KD, PARTS, DK, T], F32).ap()
        sorted_x = nc.dram_tensor("sorted_x", [STEPS * TG, D], F32).ap()
        sorted_y = nc.dram_tensor("sorted_y", [STEPS * TG, D], F32).ap()

        aw_in = [sem(f"aw_in{n}") for n in range(4)]
        ctx_in = [sem(f"ctx_in{p}") for p in range(2)]
        k_written = [sem(f"k_written{p}") for p in range(2)]
        stacked = [[sem(f"stacked{p}_{f}") for f in range(2)] for p in range(2)]
        mx_stacked = [sem(f"mx_stacked{p}") for p in range(2)]
        q_written = [sem(f"q_written{p}") for p in range(2)]
        bias_in, vo_bias_in, xr_first_in, xr_rest_in, x2_in, rw_in = (sem(n) for n in (
            "bias_in", "vo_bias_in", "xr_first_in", "xr_rest_in", "x2_in", "rw_in"))
        zeros_set, const_set, ident_set, filled = (sem(n) for n in (
            "zeros_set", "const_set", "ident_set", "filled"))
        wh_ready, wl_ready, rw_ready = (sem(n) for n in (
            "wh_ready", "wl_ready", "rw_ready"))
        ch_ready, cl_ready, keep_ready, mrow_ready = (sem(n) for n in (
            "ch_ready", "cl_ready", "keep_ready", "mrow_ready"))
        kproj_done, kf_ready, kh_ready, kl_ready = (sem(n) for n in (
            "kproj_done", "kf_ready", "kh_ready", "kl_ready"))
        vproj_done, vf_ready, vh_ready, vl_ready = (sem(n) for n in (
            "vproj_done", "vf_ready", "vh_ready", "vl_ready"))
        smax_done, max_read, maxt_done, mx_ready = (sem(n) for n in (
            "smax_done", "max_read", "maxt_done", "mx_ready"))
        st_done, pf_ready, ph_ready, pl_even, pl_odd, pv_done = (sem(n) for n in (
            "st_done", "pf_ready", "ph_ready", "pl_even", "pl_odd", "pv_done"))
        ot_ready, ott_done, rsum_ready, o_read, an_ready, at_done = (sem(n) for n in (
            "ot_ready", "ott_done", "rsum_ready", "o_read", "an_ready", "at_done"))
        th_ready, tl_ready = (sem(n) for n in (
            "th_ready", "tl_ready"))
        stats_ready, mom_ready, std_ready, rstd_ready, xn_ready = (sem(n) for n in (
            "stats_ready", "mom_ready", "std_ready", "rstd_ready", "xn_ready"))
        xt_done, xh_ready, xl_ready = (sem(n) for n in (
            "xt_done", "xh_ready", "xl_ready"))
        qproj_done, qf_ready, qh_ready, ql_ready = (sem(n) for n in (
            "qproj_done", "qf_ready", "qh_ready", "ql_ready"))
        xb_ready, oproj_done, resid_added, chain_step, xn2_ready = (sem(n) for n in (
            "xb_ready", "oproj_done", "resid_added", "chain_step", "xn2_ready"))
        ft_done, fh_ready, fl_ready, route_done = (sem(n) for n in (
            "ft_done", "fh_ready", "fl_ready", "route_done"))
        pads_set, padded, lt_ready, logits_done = (sem(n) for n in (
            "pads_set", "padded", "lt_ready", "logits_done"))
        logits_read, shifted_ready, gate_exp = (sem(n) for n in (
            "logits_read", "shifted_ready", "gate_exp"))
        h_done, hf_ready, hh_ready, hl_ready, w1h_ready, w1l_ready, w2h_ready, w2l_ready = (sem(n) for n in (
            "h_done", "hf_ready", "hh_ready", "hl_ready", "w1h_ready", "w1l_ready", "w2h_ready", "w2l_ready"))
        consts_set, tri_set, both_ready, ranked, placed, table_ready, weights_ready = (sem(n) for n in (
            "consts_set", "tri_set", "both_ready", "ranked", "placed", "table_ready", "weights_ready"))
        scattered, zero_rows, rt_done, rh_ready, rl_ready = (sem(n) for n in (
            "scattered", "zero_rows", "rt_done", "rh_ready", "rl_ready"))
        y_done, y_copied, token_done, out_written = (sem(n) for n in (
            "y_done", "y_copied", "token_done", "out_written"))
        rows_in = [sem(f"rows_in{p}") for p in range(2)]
        w1_in = [sem(f"w1_in{p}") for p in range(2)]
        w2_in = [sem(f"w2_in{p}") for p in range(2)]
        y_written = [sem(f"y_written{p}") for p in range(2)]
        chosen_in = [sem(f"chosen_in{n}") for n in range(NT)]

        v_rows = vf[:, :, :].rearrange("p k (h a d) -> p (k h) a d", a=2, d=DK)

        def v_part(b, part):
            cols = vs[b.par][:, :, :, :].rearrange("p k h n -> p (k h) n")
            return cols[:, :, DK * part:DK * part + A1 + DK].rearrange(
                "p h (a d) -> p h a d", d=DK)[:, :, 0::A1 // DK, :]

        block = ctx.enter_context(nc.Block())

        def early(b, n):
            return isinstance(b.n, int) and b.n < n

        def has(b):
            return not isinstance(b.n, int) or 0 <= b.n < B

        def is_step(t):
            return not isinstance(t.n, int) or 0 <= t.n < STEPS

        def block_rows(rows_of, t):
            return rows_of[bass.ds(TG * t.n, TG), :].rearrange("(n p) d -> p n d", p=P)

        @block.sync
        def _(sp):
            def load_ctx(b):
                if not early(b, 2):
                    sp.wait_ge(ch_ready, b.n - 1)
                    sp.wait_ge(cl_ready, b.n - 1)
                    sp.wait_ge(keep_ready, b.n - 1)
                for k in range(KD):
                    sp.dma_start(c_raw[b.par][:, k, 0:C], ctx_t[k, :, bass.ds(b.n, 1), :]
                                 .rearrange("p a n -> p (a n)")).then_inc(ctx_in[b.par], 16)
                sp.dma_start(m_raw[b.par][:, 0:C], mask[bass.ds(b.n, 1), :].to_broadcast([P, C]))\
                    .then_inc(ctx_in[b.par], 16)

            def write_keys(b):
                sp.wait_ge(kh_ready, b.n + 1)
                for c, src in enumerate((kh, kh, kl)):
                    if src is kl:
                        sp.wait_ge(kl_ready, b.n + 1)
                    for t in range(KD):
                        sp.dma_start(k_scratch[b.par][t, :, c, :, :], src[:, t, :].bitcast(F32))\
                            .then_inc(k_written[b.par], 16)

            def stack_half(b, f):
                if not early(b, 2):
                    sp.wait_ge(st_done, QUADS * (b.n - 2) + 2 * (f + 1))
                sp.wait_ge(k_written[b.par], 96 * (b.turn + 1))
                sp.wait_ge(mrow_ready, b.n + 1)
                pairs = slice(f * PAIRS // 2, (f + 1) * PAIRS // 2)
                sp.dma_start(ks[b.par][0:R_MASK, pairs, :].bitcast(F32),
                             k_scratch[b.par][f].rearrange("(q a) c d n -> (a c d) q n", a=2))\
                    .then_inc(stacked[b.par][f], 16)
                for a in range(2):
                    sp.dma_start(qs[b.par][48 * a:48 * a + 48, pairs, S * a:S * a + S].bitcast(F32),
                                 q_scratch[f, :, :, :, bass.ds(S * b.n, S)]
                                 .rearrange("(q a) c d n -> a (c d) q n", a=2)[a])\
                        .then_inc(stacked[b.par][f], 16)
                sp.dma_start(ks[b.par][R_MASK:R_MASK + 2, pairs, :].bitcast(F32),
                             m_row[b.par][:, :].bitcast(F32).rearrange("p (a n) -> p a n", a=1)
                             .to_broadcast([2, PAIRS // 2, CP])).then_inc(stacked[b.par][f], 16)

            def stack_max(b):
                sp.wait_ge(mx_ready, 2 * (b.n + 1))
                for r, src in ((0, mx_h), (1, mx_l)):
                    sp.dma_start(qs[b.par][R_MAX + r:R_MAX + r + 1, :, :].bitcast(F32)
                                 .rearrange("p q (a n) -> p (q a) n", a=2),
                                 src[:, :].bitcast(F32)).then_inc(mx_stacked[b.par], 16)

            def turn(b):
                if has(b.after(4)):
                    load_ctx(b.after(4))
                if has(b.after(2)):
                    write_keys(b.after(2))
                    stack_half(b.after(2), 0)
                if has(b.after(1)):
                    stack_max(b.after(1))
                if has(b.after(2)):
                    stack_half(b.after(2), 1)

            first = Batch(0, 0)

            def load_rows(group, done):
                sp.dma_start(xr[:, group, :], x_rows[group].rearrange("b s d -> s b d")).then_inc(done, 16)

            def load_weight(n, w):
                sp.dma_start(wraw[n], w.rearrange("k p n -> p k n")).then_inc(aw_in[n], 16)

            def write_queries(g):
                sp.wait_ge(qh_ready, g + 1)
                sp.wait_ge(ql_ready, g + 1)
                for c, src in enumerate((qh, ql, qh)):
                    for t in range(KD):
                        sp.dma_start(q_scratch[t, :, c, :, SG * g:SG * g + SG],
                                     src[g % 2][:, t, :].bitcast(F32)).then_inc(q_written[g % 2], 16)

            second = first.after(1)
            load_weight(0, wk_t)
            sp.wait_ge(zeros_set, 1)
            load_ctx(first)
            load_rows(slice(0, GB), xr_first_in)
            sp.dma_start(bk_c[:, :], bk).then_inc(bias_in, 16)
            sp.dma_start(bq_c[:, :], bq).then_inc(bias_in, 16)
            load_weight(1, wq_t)
            load_rows(slice(GB, B), xr_rest_in)
            load_weight(2, wv_t)
            sp.dma_start(bv_b[:, :], bv.to_broadcast([P, D])).then_inc(vo_bias_in, 16)
            load_ctx(second)
            load_weight(3, wo_t)
            sp.dma_start(bo_b[:, :], bo.to_broadcast([P, D])).then_inc(vo_bias_in, 16)
            sp.dma_start(rw_raw[:, :, :], router_w.rearrange("k p n -> p k n")).then_inc(rw_in, 16)
            write_keys(first)
            write_queries(0)
            sp.wait_ge(q_written[0], 96)
            sp.wait_ge(filled, 3)
            for f in range(2):
                stack_half(first, f)
            load_ctx(first.after(2))
            write_keys(second)
            write_queries(1)
            load_ctx(first.after(3))
            sp.wait_ge(filled, N_FILLS)
            write_queries(2)
            write_queries(3)
            stack_half(second, 0)
            stack_max(first)
            stack_half(second, 1)
            for p in range(2):
                sp.wait_ge(q_written[p], 96 * NG // 2)
            turn(first)
            turn(first.after(1))
            with sp.Fori(0, LOOPS) as i:
                for off in (2, 3):
                    turn(Batch(i, off))
            for b in range(2 + 2 * LOOPS, B):
                turn(Batch(0, b))

            sp.wait_ge(vproj_done, 2 * B)
            sp.dma_start(x2[:, :, :], x_tiles.rearrange("n p d -> p n d")).then_inc(x2_in, 16)
            sp.wait_ge(tri_set, 1)
            sp.dma_start(sorted_x.rearrange("(n p) d -> p n d", p=P),
                         zeros[:, :].rearrange("p (a d) -> p a d", a=1).to_broadcast([P, STEPS * TG // P, D]))\
                .then_inc(zero_rows, 16)
            sp.wait_ge(table_ready, 1)

            def table(t):
                return slice(t.n, t.n + 1) if isinstance(t.n, int) else bass.ds(t.n, 1)

            def load_w(t, part, w, low_ready, arrived):
                e = sp.value_load(expert_of[0:1, table(t)], min_val=0, max_val=E - 1)
                if not early(t, 2):
                    sp.wait_ge(low_ready, t.n - 1)
                sp.dma_start(w_raw[t.par][part][:, :, :], w[bass.ds(e, 1), :, :, :].rearrange("a k p n -> p (a k) n"))\
                    .then_inc(arrived[t.par], 16)

            def load_w1(t):
                load_w(t, 0, w1, w1l_ready, w1_in)

            def load_w2(t):
                load_w(t, 1, w2, w2l_ready, w2_in)

            def load_block(t):
                if not early(t, 2):
                    sp.wait_ge(rt_done, t.n - 1)
                sp.dma_start(rows[t.par][:, :, :], block_rows(sorted_x, t))\
                    .then_inc(rows_in[t.par], 16)

            def step(t):
                if is_step(t.after(2)):
                    load_w1(t.after(2))
                    load_block(t.after(2))
                if is_step(t.after(1)):
                    load_w2(t.after(1))

            zeroth = Batch(0, 0)
            load_w1(zeroth)
            load_w2(zeroth)
            load_w1(zeroth.after(1))
            sp.wait_ge(scattered, 16 * TOP * NT)
            load_block(zeroth)
            load_block(zeroth.after(1))
            for n in range(3):
                step(Batch(0, n))
            with sp.Fori(0, LOOP_STEPS) as i:
                for off in (3, 4):
                    step(Batch(i, off))
            for n in range(3 + 2 * LOOP_STEPS, STEPS - 1):
                step(Batch(0, n))
            for g in range(NTG):
                sp.wait_ge(token_done, TOP * (g + 1))
                sp.dma_start(out[2 * g:2 * g + 2].rearrange("n p d -> p n d"), x2[:, 2 * g:2 * g + 2, :])\
                    .then_inc(out_written, 16)
            sp.wait_ge(out_written, 16 * NTG)

        @block.gpsimd
        def _(pool):
            for p in range(2):
                pool.memset(c_raw[p][:, :, C:CP], 0.0)
                last = pool.memset(m_raw[p][:, C:CP], 0)
            last.then_inc(zeros_set, 1)
            pool.memset(eps_c[:, :], LN_EPS)
            pool.memset(ident[:, :], 0.0).then_inc(ident_set, 1)
            pool.wait_ge(ident_set, 1)
            pool.affine_select(out=ident[:, :], in_=ident[:, :], compare_op=ALU.not_equal, fill=1.0, base=0,
                               pattern=[[-1, P]], channel_multiplier=1).then_inc(ident_set, 1)
            pool.wait_ge(ident_set, 2)

            def ctx_low(b):
                pool.wait_ge(ch_ready, b.n + 1)
                pool.tensor_tensor(cl[b.par][:, :, :], c_raw[b.par][:, :, :], ch[b.par][:, :, :].bitcast(F32),
                                   ALU.subtract).then_inc(cl_ready, 1)

            def key_low(b):
                pool.wait_ge(kh_ready, b.n + 1)
                if not early(b, 1):
                    before = b.after(-1)
                    pool.wait_ge(k_written[before.par], 96 * (before.turn + 1))
                pool.tensor_tensor(kl[:, :, :], kf[:, :, :], kh[:, :, :].bitcast(F32), ALU.subtract)\
                    .then_inc(kl_ready, 1)

            def value_low(b):
                pool.wait_ge(vh_ready, b.n + 1)
                heads = [v_part(b, part) for part in range(2)]
                pool.tensor_tensor(heads[1], v_rows, heads[0].bitcast(F32), ALU.subtract).then_inc(vl_ready, 1)

            def probs_low(b, j):
                pool.wait_ge(ph_ready, QUADS * b.n + j + 1)
                pool.tensor_tensor(pl[j % 2][:, :, :], pf[j % 2][:, :, :], ph[j % 2][:, :, :].bitcast(F32),
                                   ALU.subtract).then_inc(pl_odd, 1)

            def add_parts(b):
                pool.wait_ge(o_read, 2 * (b.n + 1))
                pool.tensor_tensor(ah[:, :], ah[:, :], al[:, :], ALU.add).then_inc(an_ready, 1)

            def query_low(g):
                pool.wait_ge(qh_ready, g + 1)
                if g >= 2:
                    pool.wait_ge(q_written[g % 2], 96)
                pool.tensor_tensor(ql[g % 2][:, :, :], qf[:, :, :], qh[g % 2][:, :, :].bitcast(F32), ALU.subtract)\
                    .then_inc(ql_ready, 1)

            fills = [(ks[0][R_MASK:ROWS, :, :], 1.0), (qs[0][0:R_MASK, :, :], 0.0), (qs[0][R_MASK:ROWS, :, :], 1.0),
                     (vs[0][:, :, :, OW - 1::A1], 1.0), (vs[0][:, :, :, OW:A1], 0.0),
                     (ks[1][R_MASK:ROWS, :, :], 1.0), (qs[1][0:R_MASK, :, :], 0.0), (qs[1][R_MASK:ROWS, :, :], 1.0),
                     (vs[1][:, :, :, OW - 1::A1], 1.0), (vs[1][:, :, :, OW:A1], 0.0)]
            assert len(fills) == N_FILLS

            def fill(numbers):
                for n in numbers:
                    what, value = fills[n]
                    pool.memset(what.bitcast(F32), value).then_inc(filled, 1)
                    pool.wait_ge(filled, n + 1)

            first = Batch(0, 0)
            second = first.after(1)
            fill(range(0, 2))
            ctx_low(first)
            pool.wait_ge(cl_ready, 1)
            fill(range(2, 5))
            key_low(first)
            ctx_low(second)
            query_low(0)
            pool.wait_ge(ql_ready, 1)
            fill(range(5, 8))
            value_low(first)
            pool.wait_ge(vl_ready, 1)
            fill(range(8, N_FILLS))
            key_low(second)
            query_low(1)
            query_low(2)
            ctx_low(first.after(2))
            query_low(3)

            def turn(b):
                if has(b.after(-1)):
                    probs_low(b.after(-1), 3)
                if has(b.after(2)):
                    key_low(b.after(2))
                if has(b):
                    probs_low(b, 1)
                if has(b.after(3)):
                    ctx_low(b.after(3))
                if has(b.after(-1)):
                    add_parts(b.after(-1))
                if has(b.after(1)):
                    value_low(b.after(1))

            turn(first)
            turn(first.after(1))
            with pool.Fori(0, LOOPS) as i:
                for off in (2, 3):
                    turn(Batch(i, off))
            for b in range(2 + 2 * LOOPS, B + 1):
                turn(Batch(0, b))
            pool.wait_ge(tl_ready, B)
            pool.memset(rph[:, :, :].bitcast(F32), 0.0)
            pool.memset(rpl[:, :, :].bitcast(F32), 0.0).then_inc(pads_set, 1)
            pool.memset(ones[:, :].bitcast(F32), 1.0)
            pool.memset(both[:, NT, :].bitcast(F32), 0.0)
            pool.memset(zeros[:, :], 0.0).then_inc(tri_set, 1)
            pool.wait_ge(tri_set, 1)
            pool.affine_select(out=earlier[:, :], in_=ones[:, :].bitcast(F32), compare_op=ALU.is_gt, fill=0.0, base=0,
                               pattern=[[1, P]], channel_multiplier=-1).then_inc(tri_set, 1)
            pool.wait_ge(x2_in, 16)
            pool.wait_ge(vo_bias_in, 32)
            for g in range(NTG):
                pair = slice(2 * g, 2 * g + 2)
                pool.tensor_tensor(x2[:, pair, :], x2[:, pair, :],
                                   bo_b[:, :].rearrange("p (a n) -> p a n", a=1).to_broadcast([P, 2, D]),
                                   ALU.add).then_inc(xb_ready, 1)
            pool.wait_ge(placed, 1)
            pool.wait_ge(zero_rows, 16)
            for n in range(NT):
                for c in range(TOP):
                    pool.indirect_dma_start(sorted_x, bass.IndirectOffsetOnAxis(ap=place[c][:, n:n + 1], axis=0),
                                            xn2[:, n, :], None).then_inc(scattered, 16)

            def split_low(t, raw, high, low, ready, done):
                pool.wait_ge(ready, t.n + 1)
                pool.tensor_tensor(low[t.par][:, :, :], raw[:, :, :], high[t.par][:, :, :].bitcast(F32),
                                   ALU.subtract).then_inc(done, 1)

            def step(t):
                after = t.after(1)
                if is_step(after):
                    split_low(after, w_raw[after.par][0], w1h, w1l, w1h_ready, w1l_ready)
                if is_step(t):
                    split_low(t, w_raw[t.par][1], w2h, w2l, w2h_ready, w2l_ready)

            for n in range(-1, 3):
                step(Batch(0, n))
            with pool.Fori(0, LOOP_STEPS) as i:
                for off in (3, 4):
                    step(Batch(i, off))
            for n in range(3 + 2 * LOOP_STEPS, STEPS):
                step(Batch(0, n))
            for p in range(2):
                pool.wait_ge(y_written[p], 16 * ((STEPS + 1 - p) // 2))
            for n in range(NT):
                for c in range(TOP):
                    pool.indirect_dma_start(chosen[c][:, n, :], None, sorted_y,
                                            bass.IndirectOffsetOnAxis(ap=place[c][:, n:n + 1], axis=0))\
                        .then_inc(chosen_in[n], 16)

        @block.scalar
        def _(act):
            def attn_weight(n):
                act.wait_ge(aw_in[n], 16)
                act.copy(wh[:, n, :, :], wraw[n]).then_inc(wh_ready, 1)

            def ctx_high(b):
                act.wait_ge(ctx_in[b.par], 48 * (b.turn + 1))
                if early(b, 2):
                    act.wait_ge(zeros_set, 1)
                else:
                    act.wait_ge(vproj_done, 2 * (b.n - 1))
                act.copy(ch[b.par][:, :, :], c_raw[b.par][:, :, :]).then_inc(ch_ready, 1)

            def key_high(b):
                act.wait_ge(kf_ready, 2 * (b.n + 1))
                if not early(b, 1):
                    before = b.after(-1)
                    act.wait_ge(k_written[before.par], 96 * (before.turn + 1))
                act.copy(kh[:, :, :], kf[:, :, :]).then_inc(kh_ready, 1)

            def value_high(b):
                act.wait_ge(vf_ready, 2 * (b.n + 1))
                if not early(b, 2):
                    act.wait_ge(pv_done, QUADS * (b.n - 1))
                act.copy(v_part(b, 0), v_rows).then_inc(vh_ready, 1)

            def attn_high(b):
                act.wait_ge(at_done, b.n + 1)
                act.copy(th[:, :, bass.ds(S * b.n, S)],
                         ps[:, BK_AT, 0:KD * S].rearrange("p (k n) -> p k n", k=KD)).then_inc(th_ready, 1)

            def exps(b, j):
                act.wait_ge(st_done, QUADS * b.n + j + 1)
                again = not (early(b, 1) and j < 2)
                if again:
                    act.wait_ge((pl_even, pl_odd)[j % 2], 2 * b.n + j // 2)
                src = ps[0:CT, BK_ST:BK_ST + KT, 0:4 * S]
                act.activation(pf[j % 2][:, :, :], src, ACT.Exp).then_inc(pf_ready, 1)
                if again:
                    act.wait_ge(pv_done, QUADS * b.n + j - 1)
                act.activation(ph[j % 2][:, :, :], src, ACT.Exp).then_inc(ph_ready, 1)

            def out_copy(b, j):
                act.wait_ge(pv_done, QUADS * b.n + j + 1)
                if j == 0 and not early(b, 1):
                    act.wait_ge(ott_done, b.n)
                act.copy(ot[j][:, :], ps[0:VM, BK_OUT, 0:4 * S]).then_inc(ot_ready, 1)

            def x_std(g):
                act.wait_ge(mom_ready, GB * (g + 1))
                if g == 0:
                    act.wait_ge(ident_set, 1)
                cols = slice(GB * g, GB * (g + 1))
                act.activation(std[0:S, cols], moments[0:S, cols, 1], ACT.Sqrt, bias=eps_c[0:S, :])\
                    .then_inc(std_ready, 1)

            def x_high(g):
                act.wait_ge(xt_done, g + 1)
                if g >= 2:
                    act.wait_ge(qproj_done, 2 * (g - 1))
                act.copy(xh[g % 2][:, :, :], ps[:, 0:2, 0:SG]).then_inc(xh_ready, 1)

            def q_high(g):
                act.wait_ge(qf_ready, 2 * (g + 1))
                if g >= 2:
                    act.wait_ge(q_written[g % 2], 96)
                act.copy(qh[g % 2][:, :, :], qf[:, :, :]).then_inc(qh_ready, 1)

            first = Batch(0, 0)
            second = first.after(1)
            attn_weight(0)
            ctx_high(first)
            x_std(0)
            attn_weight(1)
            x_high(0)
            key_high(first)
            x_std(1)
            ctx_high(second)
            attn_weight(2)
            q_high(0)
            x_high(1)
            x_std(2)
            value_high(first)
            key_high(second)
            q_high(1)
            x_high(2)
            x_std(3)
            q_high(2)
            x_high(3)
            ctx_high(first.after(2))
            q_high(3)
            attn_weight(3)
            act.wait_ge(rw_in, 16)
            act.copy(rwh[:, :, :], rw_raw[:, :, :]).then_inc(rw_ready, 1)
            def turn(b):
                if has(b):
                    exps(b, 0)
                if has(b.after(-1)):
                    out_copy(b.after(-1), 2)
                if has(b.after(2)):
                    key_high(b.after(2))
                if early(b, 1):
                    for p in range(2):
                        act.wait_ge(q_written[p], 96 * NG // 2)
                if has(b):
                    exps(b, 1)
                if has(b.after(-1)):
                    out_copy(b.after(-1), 3)
                if has(b.after(3)):
                    ctx_high(b.after(3))
                if has(b):
                    exps(b, 2)
                    out_copy(b, 0)
                if has(b.after(1)):
                    value_high(b.after(1))
                if has(b):
                    exps(b, 3)
                    out_copy(b, 1)
                if has(b.after(-1)):
                    attn_high(b.after(-1))

            turn(first)
            turn(first.after(1))
            with act.Fori(0, LOOPS) as i:
                for off in (2, 3):
                    turn(Batch(i, off))
            for b in range(2 + 2 * LOOPS, B + 1):
                turn(Batch(0, b))

            def flat_high(g):
                act.wait_ge(ft_done, g + 1)
                if g >= 2:
                    act.wait_ge(route_done, g - 1)
                act.copy(fh[g % 2][:, :, :], ps[:, BK_T + g % 2, :].rearrange("p (k n) -> p k n", k=KD))\
                    .then_inc(fh_ready, 1)

            def rows_high(t):
                act.wait_ge(rt_done, t.n + 1)
                if not early(t, 2):
                    act.wait_ge(h_done, t.n - 1)
                act.copy(fh[t.par][:, :, :], ps[:, BK_T + t.par, :].rearrange("p (k n) -> p k n", k=KD))\
                    .then_inc(rh_ready, 1)

            def w1_high(t):
                act.wait_ge(w1_in[t.par], 16 * (t.turn + 1))
                if not early(t, 2):
                    act.wait_ge(h_done, t.n - 1)
                act.copy(w1h[t.par][:, :, :], w_raw[t.par][0][:, :, :]).then_inc(w1h_ready, 1)

            def silu(t):
                act.wait_ge(h_done, t.n + 1)
                if not early(t, 2):
                    act.wait_ge(hl_ready, t.n - 1)
                    act.wait_ge(y_done, t.n - 1)
                src = ps[:, 2 * t.par:2 * t.par + 2, :].rearrange("p a (b n) -> p (a b) n", b=2)
                act.activation(hf[t.par][:, :, :], src, ACT.Silu).then_inc(hf_ready, 1)
                act.activation(hh[t.par][:, :, :], src, ACT.Silu).then_inc(hh_ready, 1)

            def write_block(t):
                act.wait_ge(y_copied, t.n + 1)
                act.dma_start(block_rows(sorted_y, t), yo[t.par][:, :, :]).then_inc(y_written[t.par], 16)

            def step(t):
                if is_step(t.after(1)):
                    w1_high(t.after(1))
                if is_step(t.after(-2)):
                    write_block(t.after(-2))
                if is_step(t.after(1)):
                    rows_high(t.after(1))
                if is_step(t):
                    silu(t)

            def copy_logits_t(g):
                act.wait_ge(route_done, g + 1)
                if g >= 2:
                    act.wait_ge(logits_done, g - 1)
                act.copy(logits_t[g % 2][:, :], ps[0:E, BK_LT, 0:TG]).then_inc(lt_ready, 1)

            for g in range(NTG):
                flat_high(g)
                if g >= 1:
                    copy_logits_t(g - 1)
            copy_logits_t(NTG - 1)
            act.wait_ge(shifted_ready, 1)
            act.activation(gates[2][:, :, :], gates[1][:, :, :], ACT.Exp).then_inc(gate_exp, 1)
            for n in range(-1, 3):
                step(Batch(0, n))
            with act.Fori(0, LOOP_STEPS) as i:
                for off in (3, 4):
                    step(Batch(i, off))
            for n in range(3 + 2 * LOOP_STEPS, STEPS + 2):
                step(Batch(0, n))

        @block.vector
        def _(dve):
            def attn_weight_low(n):
                dve.wait_ge(wh_ready, n + 1)
                dve.tensor_tensor(wl[:, n, :, :], wraw[n], wh[:, n, :, :].bitcast(F32), ALU.subtract)\
                    .then_inc(wl_ready, 1)

            def masks(b):
                dve.wait_ge(ctx_in[b.par], 48 * (b.turn + 1))
                if early(b, 2):
                    dve.wait_ge(zeros_set, 1)
                else:
                    dve.wait_ge(stacked[b.par][1], 64 * b.turn)
                dve.tensor_scalar(keep[b.par][:, :], m_raw[b.par][:, :], 0.0, None, ALU.not_equal)\
                    .then_inc(keep_ready, 1)
                dve.wait_ge(keep_ready, b.n + 1)
                dve.tensor_scalar(m_row[b.par][:, :], keep[b.par][0:2, :], mask_c[:, 0:1], mask_c[:, 1:2],
                                  ALU.mult, ALU.add).then_inc(mrow_ready, 1)

            def keys(b):
                for t in range(KD):
                    dve.wait_ge(kproj_done, 2 * b.n + t + 1)
                    if t == 0 and not early(b, 1):
                        dve.wait_ge(kl_ready, b.n)
                    dve.scalar_tensor_tensor(out=kf[:, t, :], in0=ps[:, BK_KV + t, 0:CP], scalar=bk_c[:, t:t + 1],
                                             in1=keep[b.par][:, :], op0=ALU.add, op1=ALU.mult)\
                        .then_inc(kf_ready, 1)

            def values(b):
                if not early(b, 1):
                    dve.wait_ge(vl_ready, b.n)
                dve.wait_ge(vproj_done, 2 * b.n + 1)
                dve.tensor_tensor(vf[:, 0:2, :], ps[0:CT, BK_KV, :].rearrange("p (k n) -> p k n", k=2),
                                  bv_b[0:CT, :].rearrange("p (a n) -> p a n", a=1).to_broadcast([CT, 2, D]),
                                  ALU.add).then_inc(vf_ready, 1)
                dve.wait_ge(vproj_done, 2 * b.n + 2)
                dve.tensor_tensor(vf[:, 2, :], ps[0:CT, BK_KV + 1, 0:D], bv_b[0:CT, :], ALU.add)\
                    .then_inc(vf_ready, 1)

            def attn_low(b):
                dve.wait_ge(th_ready, b.n + 1)
                col = bass.ds(S * b.n, S)
                dve.tensor_tensor(tl[:, :, col], ps[:, BK_AT, 0:KD * S].rearrange("p (k n) -> p k n", k=KD),
                                  th[:, :, col].bitcast(F32), ALU.subtract).then_inc(tl_ready, 1)

            def max_rows(b):
                dve.wait_ge(maxt_done, b.n + 1)
                if not early(b, 1):
                    before = b.after(-1)
                    dve.wait_ge(mx_stacked[before.par], 32 * (before.turn + 1))
                dve.tensor_copy(mx_h[:, :], ps[0:H, BK_MAX, 0:S]).then_inc(mx_ready, 1)
                dve.wait_ge(mx_ready, 2 * b.n + 1)
                dve.tensor_tensor(mx_l[:, :], ps[0:H, BK_MAX, 0:S], mx_h[:, :].bitcast(F32), ALU.subtract)\
                    .then_inc(mx_ready, 1)

            def maxima(b, heads):
                for h in heads:
                    dve.wait_ge(smax_done, H * b.n + h + 1)
                    if h == 0 and not early(b, 1):
                        dve.wait_ge(maxt_done, b.n)
                    dve.tensor_reduce(neg_max[:, h:h + 1], ps[0:S, BK_MAX + h % 2, 0:CP], AX.X, ALU.max,
                                      negate=True).then_inc(max_read, 1)

            def probs_low(b, j):
                dve.wait_ge(ph_ready, QUADS * b.n + j + 1)
                if early(b, 1) and j == 0:
                    for p in range(2):
                        dve.wait_ge(q_written[p], 96 * NG // 2)
                dve.tensor_tensor(pl[j % 2][:, :, :], pf[j % 2][:, :, :], ph[j % 2][:, :, :].bitcast(F32),
                                  ALU.subtract).then_inc(pl_even, 1)

            def normalise(b):
                dve.wait_ge(ott_done, b.n + 1)
                o = ps[0:S, BK_KV:BK_KV + 2, 0:8 * OW].rearrange("p k (h d) -> p k h d", h=8)
                r = rsum[:, :].rearrange("p (k h) -> p k h", k=2)
                dve.reciprocal(r, o[:, :, :, 2 * DK]).then_inc(rsum_ready, 1)
                dve.wait_ge(rsum_ready, b.n + 1)
                if not early(b, 1):
                    dve.wait_ge(at_done, b.n)
                wide = rsum[:, :].rearrange("p (k h a) -> p k h a", k=2, a=1).to_broadcast([S, 2, 8, DK])
                for part, dst in ((0, ah), (1, al)):
                    dve.tensor_tensor(dst[:, :].rearrange("p (h k d) -> p k h d", k=2, h=8),
                                      o[:, :, :, DK * part:DK * (part + 1)], wide, ALU.mult).then_inc(o_read, 1)

            first = Batch(0, 0)
            dve.memset(mask_c[:, 0:1], -NEG_LO)
            dve.memset(mask_c[:, 1:2], NEG_LO).then_inc(const_set, 1)
            dve.wait_ge(const_set, 1)
            dve.memset(mask_c[0:1, 0:1], -NEG_HI)
            for e in range(E):
                dve.memset(pos[:, :, e:e + 1], float(E - e))
            dve.memset(mask_c[0:1, 1:2], NEG_HI).then_inc(const_set, 1)
            dve.wait_ge(const_set, 2)

            def x_stats(g):
                dve.wait_ge(xr_rest_in if g else xr_first_in, 16)
                for b in range(GB * g, GB * (g + 1)):
                    dve.bn_stats(stats[0:S, b, :], xr[:, b, :]).then_inc(stats_ready, 1)
                for b in range(GB * g, GB * (g + 1)):
                    dve.wait_ge(stats_ready, b + 1)
                    dve.bn_aggr(moments[0:S, b, :], stats[0:S, b, :]).then_inc(mom_ready, 1)

            def normalise_x(g):
                dve.wait_ge(std_ready, g + 1)
                cols = slice(GB * g, GB * (g + 1))
                dve.reciprocal(rstd[0:S, cols], std[0:S, cols]).then_inc(rstd_ready, 1)
                dve.wait_ge(rstd_ready, g + 1)
                for b in range(GB * g, GB * (g + 1)):
                    dve.tensor_scalar(xr[:, b, :], xr[:, b, :], moments[0:S, b, 0:1], rstd[0:S, b:b + 1],
                                      ALU.subtract, ALU.mult).then_inc(xn_ready, 1)

            def x_low(g):
                dve.wait_ge(xh_ready, g + 1)
                dve.tensor_tensor(xl[g % 2][:, :, :], ps[:, 0:2, 0:SG], xh[g % 2][:, :, :].bitcast(F32),
                                  ALU.subtract).then_inc(xl_ready, 1)

            def queries(g):
                for t in range(KD):
                    dve.wait_ge(qproj_done, 2 * g + t + 1)
                    if g and t == 0:
                        dve.wait_ge(ql_ready, g)
                    dve.tensor_scalar(qf[:, t, :], ps[:, (2, BK_OUT)[t], 0:SG], bq_c[:, t:t + 1], DK ** -0.5,
                                      ALU.add, ALU.mult).then_inc(qf_ready, 1)

            second, third = first.after(1), first.after(2)
            attn_weight_low(0)
            x_stats(0)
            masks(first)
            normalise_x(0)
            dve.wait_ge(bias_in, 32)
            keys(first)
            attn_weight_low(1)
            x_low(0)
            x_stats(1)
            normalise_x(1)
            queries(0)
            attn_weight_low(2)
            x_low(1)
            dve.wait_ge(vo_bias_in, 32)
            values(first)
            x_stats(2)
            normalise_x(2)
            masks(second)
            keys(second)
            queries(1)
            x_low(2)
            maxima(first, range(0, 8))
            x_stats(3)
            normalise_x(3)
            queries(2)
            x_low(3)
            queries(3)
            maxima(first, range(8, H))
            max_rows(first)
            masks(third)
            keys(third)
            attn_weight_low(3)
            dve.wait_ge(rw_ready, 1)
            dve.tensor_tensor(rwl[:, :, :], rw_raw[:, :, :], rwh[:, :, :].bitcast(F32), ALU.subtract)\
                .then_inc(rw_ready, 1)

            def turn(b):
                after, before = b.after(1), b.after(-1)
                if has(after):
                    maxima(after, range(0, 8))
                if has(b):
                    probs_low(b, 0)
                if has(after):
                    maxima(after, range(8, 10))
                    values(after)
                    maxima(after, range(10, H))
                    max_rows(after)
                if has(before):
                    normalise(before)
                if has(b):
                    probs_low(b, 2)
                if has(b.after(3)):
                    masks(b.after(3))
                if has(before):
                    attn_low(before)
                if has(b.after(3)):
                    keys(b.after(3))

            turn(first)
            turn(first.after(1))
            with dve.Fori(0, LOOPS) as i:
                for off in (2, 3):
                    turn(Batch(i, off))
            for b in range(2 + 2 * LOOPS, B + 1):
                turn(Batch(0, b))

            n_steps = [0]

            def step(ins):
                n_steps[0] += 1
                ins.then_inc(chain_step, 1)
                dve.wait_ge(chain_step, n_steps[0])

            def residual(g):
                dve.wait_ge(oproj_done, g + 1)
                dve.wait_ge(xb_ready, g + 1)
                dve.tensor_tensor(x2[:, 2 * g:2 * g + 2, :], ps[:, g, :].rearrange("p (n d) -> p n d", n=2),
                                  x2[:, 2 * g:2 * g + 2, :], ALU.add).then_inc(resid_added, 1)
                if g >= 1:
                    row_stats(g - 1)

            def row_stats(g):
                dve.wait_ge(resid_added, g + 1)
                for n in (2 * g, 2 * g + 1):
                    last = dve.bn_stats(st2[:, n, :], x2[:, n, :])
                if g == NTG - 1:
                    step(last)

            def all_rstd():
                for n in range(NT):
                    last = dve.bn_aggr(mo2[:, n, :], st2[:, n, :])
                step(last)
                var, r, t, u = nw
                step(dve.tensor_scalar(var[:, :], mo2[:, :, 1], LN_EPS, None, ALU.add))
                step(dve.tensor_scalar(t[:, :].bitcast(I32), var[:, :].bitcast(I32), 1, None,
                                       ALU.logical_shift_right))
                step(dve.tensor_scalar(r[:, :].bitcast(I32), t[:, :].bitcast(I32), -1.0, float(MAGIC),
                                       ALU.mult, ALU.add))
                for _ in range(4):
                    step(dve.tensor_tensor(t[:, :], r[:, :], r[:, :], ALU.mult))
                    step(dve.scalar_tensor_tensor(out=u[:, :], in0=t[:, :], scalar=-0.5, in1=var[:, :],
                                                  op0=ALU.mult, op1=ALU.mult))
                    step(dve.scalar_tensor_tensor(out=r[:, :], in0=u[:, :], scalar=1.5, in1=r[:, :],
                                                  op0=ALU.add, op1=ALU.mult))

            def normalise_rows(g):
                for n in (2 * g, 2 * g + 1):
                    last = dve.tensor_scalar(xn2[:, n, :], x2[:, n, :], mo2[:, n, 0:1], nw[1][:, n:n + 1],
                                             ALU.subtract, ALU.mult)
                last.then_inc(xn2_ready, 1)

            def flat_low(g):
                dve.wait_ge(fh_ready, g + 1)
                dve.tensor_tensor(fl[g % 2][:, :, :], ps[:, BK_T + g % 2, :].rearrange("p (k n) -> p k n", k=KD),
                                  fh[g % 2][:, :, :].bitcast(F32), ALU.subtract).then_inc(fl_ready, 1)

            logits, shifted, expd, picked, rest, t0, t1, second, cw = gates
            c0, c1, c2, c3 = gcol

            def wide2(col):
                return col[:, :].rearrange("p (n a) -> p n a", a=1).to_broadcast([P, NT, E])

            def first_of(src, col, dst):
                step(dve.tensor_tensor(t0[:, :, :], src, wide2(col), ALU.is_equal))
                step(dve.tensor_tensor(t1[:, :, :], t0[:, :, :], pos[:, :, :], ALU.mult))
                step(dve.tensor_reduce(c1[:, :], t1[:, :, :], AX.X, ALU.max))
                step(dve.tensor_tensor(dst, t1[:, :, :], wide2(c1), ALU.is_equal))

            def find_first():
                dve.wait_ge(logits_done, NTG)
                dve.tensor_copy(logits[:, :, :], ps[:, BK_L, 0:NT * E].rearrange("p (n e) -> p n e", n=NT))\
                    .then_inc(logits_read, 1)
                dve.wait_ge(logits_read, 1)
                step(dve.tensor_reduce(c0[:, :], logits[:, :, :], AX.X, ALU.max))
                dve.tensor_tensor(shifted[:, :, :], logits[:, :, :], wide2(c0), ALU.subtract)\
                    .then_inc(shifted_ready, 1)
                first_of(logits[:, :, :], c0, picked[:, :, :])

            def find_second():
                step(dve.scalar_tensor_tensor(out=rest[:, :, :], in0=picked[:, :, :], scalar=-3.0e38,
                                              in1=logits[:, :, :], op0=ALU.mult, op1=ALU.add))
                step(dve.tensor_reduce(c2[:, :], rest[:, :, :], AX.X, ALU.max))
                first_of(rest[:, :, :], c2, second[:, :, :])
                dve.wait_ge(tri_set, 1)
                dve.tensor_tensor(both[:, 0:NT, :], picked[:, :, :], second[:, :, :], ALU.add)\
                    .then_inc(both_ready, 1)
                dve.wait_ge(both_ready, 1)

            def place_rows():
                dve.wait_ge(ranked, 1)
                step(dve.tensor_copy(counts[:, :], ps[:, BK_RANK, NT * E:(NT + 1) * E]))
                step(dve.tensor_tensor(is_block[:, :, :], counts[:, :].rearrange("p (e a) -> p e a", a=1)
                                       .to_broadcast([P, E, T // TG]), block_start[:, :, :], ALU.is_gt))
                step(dve.tensor_reduce(blocks[:, :], is_block[:, :, :], AX.X, ALU.add))
                step(dve.tensor_tensor(blocks_to[:, :, :], blocks[:, :].rearrange("p (a e) -> p a e", a=1)
                                       .to_broadcast([P, E, E]), up_to[:, :, :], ALU.mult))
                step(dve.tensor_reduce(block_end[:, :], blocks_to[:, :, :], AX.X, ALU.add))
                step(dve.tensor_tensor(blocks_before[:, :], block_end[:, :], blocks[:, :], ALU.subtract))
                step(dve.tensor_scalar(first_row[:, :], blocks_before[:, :], float(TG), None, ALU.mult))
                step(dve.tensor_tensor(t0[:, :, :], ps[:, BK_RANK, 0:NT * E].rearrange("p (n e) -> p n e", n=NT),
                                       first_row[:, :].rearrange("p (a e) -> p a e", a=1).to_broadcast([P, NT, E]),
                                       ALU.add))
                for one_of, c, dst in ((picked, c0, place[0]), (second, c1, place[1])):
                    step(dve.tensor_tensor(t1[:, :, :], t0[:, :, :], one_of[:, :, :], ALU.mult))
                    step(dve.tensor_reduce(c[:, :], t1[:, :, :], AX.X, ALU.add))
                    last = dve.tensor_copy(dst[:, :], c[:, :])
                last.then_inc(placed, 1)

            def plan_steps():
                step(dve.tensor_tensor(passed[:, :, :], block_end[0:1, :].rearrange("p (a e) -> p a e", a=1)
                                       .to_broadcast([1, STEPS, E]), step_no[:, :, :], ALU.is_le))
                step(dve.tensor_reduce(step_expert[:, :], passed[:, :, :], AX.X, ALU.add))
                step(dve.tensor_scalar(step_expert[:, :], step_expert[:, :], float(E - 1), None, ALU.min))
                dve.tensor_copy(expert_of[:, :], step_expert[:, :]).then_inc(table_ready, 1)

            def weigh():
                dve.wait_ge(gate_exp, 1)
                step(dve.tensor_reduce(c0[:, :], expd[:, :, :], AX.X, ALU.add))
                step(dve.reciprocal(c1[:, :], c0[:, :]))
                step(dve.tensor_tensor(t0[:, :, :], expd[:, :, :], wide2(c1), ALU.mult))
                step(dve.tensor_tensor(t1[:, :, :], t0[:, :, :], both[:, 0:NT, :].bitcast(F32), ALU.mult))
                step(dve.tensor_reduce(c2[:, :], t1[:, :, :], AX.X, ALU.add))
                step(dve.tensor_scalar(c3[:, :], c2[:, :], GATE_EPS, None, ALU.max))
                step(dve.reciprocal(c0[:, :], c3[:, :]))
                step(dve.tensor_tensor(cw[:, :, :], t1[:, :, :], wide2(c0), ALU.mult))
                for one_of, w in ((picked, weight[0]), (second, weight[1])):
                    step(dve.tensor_tensor(t0[:, :, :], cw[:, :, :], one_of[:, :, :], ALU.mult))
                    step(dve.tensor_reduce(w[:, :], t0[:, :, :], AX.X, ALU.add))

            def rows_low(t):
                dve.wait_ge(rh_ready, t.n + 1)
                dve.tensor_tensor(fl[t.par][:, :, :], ps[:, BK_T + t.par, :].rearrange("p (k n) -> p k n", k=KD),
                                  fh[t.par][:, :, :].bitcast(F32), ALU.subtract).then_inc(rl_ready, 1)

            def w2_high(t):
                dve.wait_ge(w2_in[t.par], 16 * (t.turn + 1))
                if not early(t, 2):
                    dve.wait_ge(y_done, t.n - 1)
                dve.tensor_copy(w2h[t.par][:, :, :], w_raw[t.par][1][:, :, :]).then_inc(w2h_ready, 1)

            def h_low(t):
                dve.wait_ge(hh_ready, t.n + 1)
                dve.tensor_tensor(hl[t.par][:, :, :], hf[t.par][:, :, :], hh[t.par][:, :, :].bitcast(F32),
                                  ALU.subtract).then_inc(hl_ready, 1)

            def copy_y(t):
                dve.wait_ge(y_done, t.n + 1)
                if not early(t, 2):
                    dve.wait_ge(y_written[t.par], 16 * t.turn)
                dve.tensor_copy(yo[t.par][:, :, :], ps[:, BK_Y + t.par, :].rearrange("p (n d) -> p n d", n=2))\
                    .then_inc(y_copied, 1)

            def expert_step(t):
                if is_step(t.after(1)):
                    rows_low(t.after(1))
                if is_step(t):
                    h_low(t)
                if is_step(t.after(-1)):
                    copy_y(t.after(-1))
                if is_step(t.after(1)):
                    w2_high(t.after(1))

            for b in range(T // TG):
                dve.memset(block_start[:, :, b:b + 1], float(TG * b))
            for e in range(E):
                dve.memset(up_to[:, e, 0:e + 1], 1.0)
                if e + 1 < E:
                    dve.memset(up_to[:, e, e + 1:E], 0.0)
            for n in range(STEPS):
                last = dve.memset(step_no[:, n, :], float(n))
            last.then_inc(consts_set, 1)
            dve.wait_ge(consts_set, 1)
            dve.wait_ge(pads_set, 1)
            for padded_w, w in ((rph, rwh), (rpl, rwl)):
                dve.tensor_copy(padded_w[:, :, 0:E], w[:, :, :].bitcast(F32)).then_inc(padded, 1)
            for g in range(NTG):
                residual(g)
            row_stats(NTG - 1)
            all_rstd()
            normalise_rows(0)
            normalise_rows(1)
            for g in range(NTG):
                flat_low(g)
                if g + 2 < NTG:
                    normalise_rows(g + 2)
            find_first()
            find_second()
            place_rows()
            plan_steps()
            weigh()
            for n in range(-1, 3):
                expert_step(Batch(0, n))
            with dve.Fori(0, LOOP_STEPS) as i:
                for off in (3, 4):
                    expert_step(Batch(i, off))
            for n in range(3 + 2 * LOOP_STEPS, STEPS + 1):
                expert_step(Batch(0, n))
            for n in range(NT):
                dve.wait_ge(chosen_in[n], 16 * TOP)
                for c in range(TOP):
                    last = dve.scalar_tensor_tensor(out=x2[:, n, :], in0=chosen[c][:, n, :],
                                                    scalar=weight[c][:, n:n + 1], in1=x2[:, n, :],
                                                    op0=ALU.mult, op1=ALU.add)
                    if c + 1 < TOP:
                        step(last)
                last.then_inc(token_done, 1)

        @block.tensor
        def _(pe):
            def product(o, terms):
                for n, (lhs, rhs) in enumerate(terms):
                    last = pe.matmul(o, lhs, rhs, start=n == 0, stop=n == len(terms) - 1)
                return last

            def project_keys(b, t):
                if t == 0:
                    pe.wait_ge(ch_ready, b.n + 1)
                    pe.wait_ge(cl_ready, b.n + 1)
                    if early(b, 4):
                        if b.n:
                            pe.wait_ge(*{1: (vf_ready, 2), 2: (kf_ready, 4), 3: (vf_ready, 4)}[b.n])
                    else:
                        pe.wait_ge(o_read, 2 * (b.n - 3))
                m = slice(t * P, (t + 1) * P)
                product(ps[:, BK_KV + t, 0:CP],
                        [(w[:, 0, k, m], c[b.par][:, k, :]) for k in range(KD)
                         for w, c in ((wh, ch), (wl, ch), (wh, cl))]).then_inc(kproj_done, 1)

            def project_values(b, k3):
                if k3 == 0:
                    if early(b, 1):
                        pe.wait_ge(kf_ready, 2)
                    elif has(b.after(1)):
                        pe.wait_ge(kf_ready, 2 * (b.n + 2))
                    else:
                        pe.wait_ge(o_read, 2 * (b.n - 2))
                m = slice(k3 * CT, (k3 + 1) * CT)
                last = product(ps[0:CT, BK_KV + k3 // 2, D * (k3 % 2):D * (k3 % 2) + D],
                               [(c[b.par][:, k, m], w[:, 2, k, :]) for k in range(KD)
                                for w, c in ((wh, ch), (wh, cl), (wl, ch))])
                if k3 != 0:
                    last.then_inc(vproj_done, 1)

            def head_scores(b, heads):
                for h in heads:
                    if h % HALF == 0:
                        pe.wait_ge(stacked[b.par][h // HALF], 64 * (b.turn + 1))
                    if h >= 2:
                        pe.wait_ge(max_read, H * b.n + h - 1)
                    elif h == 0 and not early(b, 1):
                        pe.wait_ge(mx_ready, 2 * b.n)
                    elif h == 1 and not early(b, 3):
                        pe.wait_ge(tl_ready, b.n - 2)
                    pe.matmul(ps[0:S, BK_MAX + h % 2, 0:CP],
                              qs[b.par][0:R_MAX, h // 2, S * (h % 2):S * (h % 2) + S],
                              ks[b.par][0:R_MAX, h // 2, :], start=True, stop=True).then_inc(smax_done, 1)

            def max_transpose(b):
                pe.wait_ge(max_read, H * (b.n + 1))
                pe.transpose(ps[0:H, BK_MAX, 0:S], neg_max[:, :], ident[0:S, 0:S]).then_inc(maxt_done, 1)

            def quad_scores(b, j):
                if j == 0:
                    pe.wait_ge(mx_stacked[b.par], 32 * (b.turn + 1))
                if not (early(b, 1) and j < 1):
                    pe.wait_ge(ph_ready, QUADS * b.n + j)
                for k3 in range(KT):
                    for q in range(2):
                        last = pe.matmul(ps[0:CT, BK_ST + k3, 2 * S * q:2 * S * (q + 1)],
                                         ks[b.par][0:ROWS, 2 * j + q, k3 * CT:(k3 + 1) * CT],
                                         qs[b.par][0:ROWS, 2 * j + q, :], start=True, stop=True)
                last.then_inc(st_done, 1)

            def quad_outputs(b, j, q):
                if q == 0:
                    pe.wait_ge((pl_even, pl_odd)[j % 2], 2 * b.n + j // 2 + 1)
                    if j == 0:
                        pe.wait_ge(vl_ready, b.n + 1)
                    if not (early(b, 1) and j < 1):
                        pe.wait_ge(ot_ready, QUADS * b.n + j)
                cols = slice(2 * S * q, 2 * S * (q + 1))
                last = product(ps[0:VM, BK_OUT, cols],
                               [(vs[b.par][:, k3, 2 * j + q, 0:VM], part[j % 2][:, k3, cols])
                                for k3 in range(KT) for part in (ph, pl)])
                if q == 1:
                    last.then_inc(pv_done, 1)

            def out_transpose(b):
                pe.wait_ge(ot_ready, QUADS * (b.n + 1))
                if has(b.after(2)):
                    pe.wait_ge(vf_ready, 2 * (b.n + 3))
                else:
                    pe.wait_ge(o_read, 2 * b.n)
                for h in range(H):
                    rows = slice(A1 * (h % 2), A1 * (h % 2) + OW) if h else slice(0, VM)
                    c = OW * (h // 2)
                    last = pe.transpose(ps[0:S, BK_KV + h % 2, c:c + rows.stop - rows.start],
                                        ot[h // 4][rows, S * (h % 4):S * (h % 4 + 1)], ident[rows, rows])
                last.then_inc(ott_done, 1)

            def attn_transpose(b):
                pe.wait_ge(an_ready, b.n + 1)
                if not has(b.after(2)):
                    pe.wait_ge(tl_ready, b.n)
                for k in range(KD):
                    last = pe.transpose(ps[:, BK_AT, S * k:S * (k + 1)], ah[:, k * P:(k + 1) * P], ident[0:S, 0:S])
                last.then_inc(at_done, 1)

            def turn(b):
                after, before = b.after(1), b.after(-1)

                def heads(*numbers):
                    if has(after):
                        head_scores(after, numbers)

                heads(0)
                if has(b):
                    quad_scores(b, 0)
                heads(1)
                if has(before):
                    quad_outputs(before, 2, 0)
                heads(2)
                if has(before):
                    quad_outputs(before, 2, 1)
                heads(3)
                if has(after):
                    project_values(after, 0)
                heads(4)
                if has(after):
                    project_values(after, 1)
                heads(5)
                if has(b):
                    quad_scores(b, 1)
                heads(6)
                if has(before):
                    quad_outputs(before, 3, 0)
                heads(7)
                if has(before):
                    quad_outputs(before, 3, 1)
                heads(8)
                if has(after):
                    project_values(after, 2)
                heads(9)
                if has(b):
                    quad_scores(b, 2)
                heads(10)
                if has(b):
                    quad_outputs(b, 0, 0)
                heads(11)
                if has(b):
                    quad_outputs(b, 0, 1)
                heads(12)
                if has(before):
                    out_transpose(before)
                heads(13)
                if has(b):
                    quad_scores(b, 3)
                heads(14, 15)
                if has(after):
                    max_transpose(after)
                if has(b):
                    quad_outputs(b, 1, 0)
                    quad_outputs(b, 1, 1)
                if has(b.after(3)):
                    project_keys(b.after(3), 0)
                if has(before):
                    attn_transpose(before)
                if has(b.after(3)):
                    project_keys(b.after(3), 1)

            first = Batch(0, 0)

            def x_transpose(g):
                pe.wait_ge(xn_ready, GB * (g + 1))
                if g == 0:
                    pe.wait_ge(ident_set, 2)
                else:
                    pe.wait_ge(xl_ready, g)
                for k in range(KD):
                    for b in range(GB):
                        last = pe.transpose(ps[:, k, S * b:S * (b + 1)], xr[:, GB * g + b, k * P:(k + 1) * P],
                                            ident[0:S, 0:S])
                last.then_inc(xt_done, 1)

            def project_queries(g):
                pe.wait_ge(wl_ready, 2)
                pe.wait_ge(xl_ready, g + 1)
                for t in range(KD):
                    if g >= 1:
                        pe.wait_ge(qf_ready, 2 * g - 1 + t)
                    m = slice(t * P, (t + 1) * P)
                    product(ps[:, (2, BK_OUT)[t], 0:SG],
                            [(w[:, 1, k, m], x[g % 2][:, k, :]) for k in range(KD)
                             for w, x in ((wh, xh), (wl, xh), (wh, xl))]).then_inc(qproj_done, 1)

            pe.wait_ge(wl_ready, 1)
            for t in range(KD):
                project_keys(first, t)
            x_transpose(0)
            project_queries(0)
            x_transpose(1)
            pe.wait_ge(wl_ready, 3)
            for k3 in range(KT):
                project_values(first, k3)
            for t in range(KD):
                project_keys(first.after(1), t)
            project_queries(1)
            x_transpose(2)
            pe.wait_ge(filled, 3)
            head_scores(first, range(0, 8))
            project_queries(2)
            x_transpose(3)
            project_queries(3)
            head_scores(first, range(8, H))
            max_transpose(first)
            for t in range(KD):
                project_keys(first.after(2), t)
            pe.wait_ge(filled, N_FILLS)
            pe.wait_ge(qf_ready, KD * NG)
            turn(first)
            turn(first.after(1))
            with pe.Fori(0, LOOPS) as i:
                for off in (2, 3):
                    turn(Batch(i, off))
            for b in range(2 + 2 * LOOPS, B + 1):
                turn(Batch(0, b))

            def project_output(g):
                for a in range(2):
                    m = slice((2 * g + a) * P, (2 * g + a + 1) * P)
                    last = product(ps[:, g, D * a:D * (a + 1)],
                                   [(x[:, k, m], w[:, 3, k, :]) for k in range(KD)
                                    for x, w in ((th, wh), (th, wl), (tl, wh))])
                last.then_inc(oproj_done, 1)

            def flat_transpose(g):
                pe.wait_ge(xn2_ready, g + 1)
                if g >= 2:
                    pe.wait_ge(fl_ready, g - 1)
                for k in range(KD):
                    for a in range(2):
                        last = pe.transpose(ps[:, BK_T + g % 2, TG * k + P * a:TG * k + P * (a + 1)],
                                            xn2[:, 2 * g + a, k * P:(k + 1) * P], ident[:, :])
                last.then_inc(ft_done, 1)

            def route(g):
                pe.wait_ge(fl_ready, g + 1)
                if g >= 1:
                    pe.wait_ge(lt_ready, g)
                product(ps[:, BK_LT, 0:TG],
                        [(w[:, k, :], f[g % 2][:, k, :]) for k in range(KD)
                         for w, f in ((rph, fh), (rpl, fh), (rph, fl))]).then_inc(route_done, 1)

            def logits_back(g):
                pe.wait_ge(lt_ready, g + 1)
                for a in range(2):
                    n = 2 * g + a
                    last = pe.transpose(ps[:, BK_L, E * n:E * (n + 1)], logits_t[g % 2][:, a * P:(a + 1) * P],
                                        ident[0:E, 0:E])
                last.then_inc(logits_done, 1)

            def rank():
                pe.wait_ge(tri_set, 2)
                pe.wait_ge(both_ready, 1)
                wide = (NT + 1) * E
                pe.matmul(ps[:, BK_RANK, 0:wide], earlier[:, :], both[:, :, :].rearrange("p n e -> p (n e)"),
                          start=True, stop=False)
                for n in range(NT):
                    last = pe.matmul(ps[:, BK_RANK, (n + 1) * E:wide].rearrange("p (n e) -> p n e", e=E), ones[:, :],
                                     both[:, n:n + 1, :].to_broadcast([P, NT - n, E]), start=False, stop=n == NT - 1)
                last.then_inc(ranked, 1)

            def rows_transpose(t):
                pe.wait_ge(rows_in[t.par], 16 * (t.turn + 1))
                if not early(t, 2):
                    pe.wait_ge(rl_ready, t.n - 1)
                for k in range(KD):
                    for a in range(2):
                        last = pe.transpose(ps[:, BK_T + t.par, TG * k + P * a:TG * k + P * (a + 1)],
                                            rows[t.par][:, a, k * P:(k + 1) * P], ident[:, :])
                last.then_inc(rt_done, 1)

            def hidden(t):
                pe.wait_ge(rl_ready, t.n + 1)
                pe.wait_ge(w1l_ready, t.n + 1)
                if not early(t, 2):
                    pe.wait_ge(hh_ready, t.n - 1)
                for f in range(KF):
                    c = slice(f * P, (f + 1) * P)
                    last = product(ps[:, 2 * t.par + f // 2, TG * (f % 2):TG * (f % 2 + 1)],
                                   [(w[t.par][:, k, c], x[t.par][:, k, :]) for k in range(KD)
                                    for w, x in ((w1h, fh), (w1l, fh), (w1h, fl))])
                last.then_inc(h_done, 1)

            def expert_out(t):
                pe.wait_ge(hl_ready, t.n + 1)
                pe.wait_ge(w2l_ready, t.n + 1)
                if not early(t, 2):
                    pe.wait_ge(y_copied, t.n - 1)
                for a in range(2):
                    m = slice(a * P, (a + 1) * P)
                    last = product(ps[:, BK_Y + t.par, D * a:D * (a + 1)],
                                   [(x[t.par][:, f, m], w[t.par][:, f, :]) for f in range(KF)
                                    for x, w in ((hh, w2h), (hh, w2l), (hl, w2h))])
                last.then_inc(y_done, 1)

            def step(t):
                if is_step(t):
                    hidden(t)
                if is_step(t.after(1)):
                    rows_transpose(t.after(1))
                if is_step(t.after(-1)):
                    expert_out(t.after(-1))

            pe.wait_ge(wl_ready, 4)
            pe.wait_ge(th_ready, B)
            pe.wait_ge(tl_ready, B)
            for g in range(NTG):
                project_output(g)
            pe.wait_ge(padded, 2)
            for g in range(NTG):
                flat_transpose(g)
                if g >= 1:
                    route(g - 1)
                if g >= 2:
                    logits_back(g - 2)
            route(NTG - 1)
            logits_back(NTG - 2)
            logits_back(NTG - 1)
            rank()
            for n in range(-1, 3):
                step(Batch(0, n))
            with pe.Fori(0, LOOP_STEPS) as i:
                for off in (3, 4):
                    step(Batch(i, off))
            for n in range(3 + 2 * LOOP_STEPS, STEPS + 1):
                step(Batch(0, n))


def kernel(x, ctx_1024, mask_BxS2_ik0, L0_xattn_Wq, L0_xattn_bq, L0_xattn_Wk, L0_xattn_bk, L0_xattn_Wv,
           L0_xattn_bv, L0_xattn_Wo, L0_xattn_bo, L0_ffn_router_w, L0_ffn_w1, L0_ffn_w2):
    import numpy as np
    import concourse.bacc as bacc
    from concourse.bass_utils import run_bass_kernel_spmd

    def halves(w):
        return np.ascontiguousarray(np.asarray(w)).reshape(KD, P, -1)

    x = np.asarray(x)
    arrays = {
        "x_rows": x,
        "x_tiles": x.reshape(NT, P, D),
        "ctx_t": np.ascontiguousarray(np.asarray(ctx_1024).transpose(2, 0, 1)).reshape(KD, P, B, C),
        "mask": np.asarray(mask_BxS2_ik0),
        "wq_t": halves(np.asarray(L0_xattn_Wq).T),
        "wk_t": halves(np.asarray(L0_xattn_Wk).T),
        "wv_t": halves(np.asarray(L0_xattn_Wv).T),
        "wo_t": halves(np.asarray(L0_xattn_Wo).T),
        "bq": np.ascontiguousarray(np.asarray(L0_xattn_bq).reshape(KD, P).T),
        "bk": np.ascontiguousarray(np.asarray(L0_xattn_bk).reshape(KD, P).T),
        "bv": np.asarray(L0_xattn_bv).reshape(1, D),
        "bo": np.asarray(L0_xattn_bo).reshape(1, D),
        "router_w": halves(L0_ffn_router_w),
        "w1": np.ascontiguousarray(np.asarray(L0_ffn_w1)).reshape(E, KD, P, F),
        "w2": np.ascontiguousarray(np.asarray(L0_ffn_w2)).reshape(E, KF, P, D),
    }
    nc = bacc.Bacc("TRN2", target_bir_lowering=False, num_devices=1)
    args = [nc.dram_tensor(n, a.shape, mybir.dt.from_np(a.dtype), kind="ExternalInput").ap()
            for n, a in arrays.items()]
    args.append(nc.dram_tensor("out", (NT, P, D), F32, kind="ExternalOutput").ap())
    xattn_moe_kernel(nc, *args)
    r = run_bass_kernel_spmd(nc, [arrays], core_ids=[0])
    return np.asarray(r.results[0]["out"]).reshape(B, S, D)
```
